# Optimizing a Trainium2 kernel written in Bass

```python
import numpy as np
import jax
import jax.numpy as jnp

def _softmax(x, axis=-1):
    return jax.nn.softmax(x, axis=axis)
def _gelu(x):
    return jax.nn.gelu(x, approximate=True)
def _silu(x):
    return jax.nn.silu(x)
def _sigmoid(x):
    return jax.nn.sigmoid(x)
def _layernorm(x, axis=-1, eps=1e-5):
    m = jnp.mean(x, axis=axis, keepdims=True)
    v = jnp.var(x, axis=axis, keepdims=True)
    return (x - m) / jnp.sqrt(v + eps)
def _scatter_add(tgt, idx, src, axis=0):
    return tgt.at[idx].add(src)
def _segment_sum(src, seg, n):
    return jax.ops.segment_sum(src, seg, n)

kernel_name = 'mk_conv_seq_d4_conv_nchw128_e1eb27'

def setup_inputs(seed: int = 0):
    np.random.seed(seed)
    _w = jnp.asarray
    def _rec_inputs():
        import jax
        import jax.numpy as jnp
        _gk = jax.random.key(seed)
        x = -0.0005207 + 1.001 * jax.random.normal(jax.random.fold_in(_gk, 1), (4, 128, 64, 64), jnp.float32)
        return x
    x = _rec_inputs()
    def _L0_conv_setup():
        import jax, jax.numpy as jnp
        import numpy as np
        C = 128
        MID = C // 4
        H = W = 64
        B = 4
        SOFTMAX_SCALE = 1.0

        def _leaky(z):
            return jnp.where(z >= 0, z, 0.2 * z)

        def _conv1x1(x, w, b):
            return jnp.einsum('oc,bchw->bohw', w, x) + b[None, :, None, None]

        def _attn_sample(q_map, v_map, w_map, b_map):
            n = H * W
            q = q_map.reshape(C, n)
            v = v_map.reshape(C, n)
            w = w_map.reshape(n)
            b = b_map.reshape(n)
            norm = jnp.sqrt(jnp.sum(q * q, axis=0))
            k = q / jnp.clip(norm, 0.0001)[None, :]
            logits = jnp.einsum('cn,cm->nm', k, q)
            mean = jnp.mean(logits, axis=0, keepdims=True)
            sparse = jax.nn.relu(logits - mean * w[None, :] + b[None, :])
            mask = (sparse != 0.0).astype(logits.dtype)
            attn = jax.nn.softmax(logits * sparse * SOFTMAX_SCALE, axis=0)
            attn = jnp.clip(attn * mask, 1e-08)
            out = jnp.einsum('cn,nm->cm', v, attn)
            return out.reshape(C, H, W)
        key = jax.random.key(seed)
        ks = jax.random.split(key, 16)
        s = 0.05
        inp = {'x': jax.random.normal(ks[0], (B, C, H, W), dtype=jnp.float32), 'q_w': jax.random.normal(ks[1], (C, C), dtype=jnp.float32) * s, 'q_b': jnp.zeros((C,), dtype=jnp.float32), 'v_w': jax.random.normal(ks[2], (C, C), dtype=jnp.float32) * s, 'v_b': jnp.zeros((C,), dtype=jnp.float32), 'lw1_w': jax.random.normal(ks[3], (MID, C), dtype=jnp.float32) * s, 'lw1_b': jnp.zeros((MID,), dtype=jnp.float32), 'lw2_w': jax.random.normal(ks[4], (1, MID), dtype=jnp.float32) * s, 'lw2_b': jnp.zeros((1,), dtype=jnp.float32), 'bw1_w': jax.random.normal(ks[5], (MID, C), dtype=jnp.float32) * s, 'bw1_b': jnp.zeros((MID,), dtype=jnp.float32), 'bw2_w': jax.random.normal(ks[6], (1, MID), dtype=jnp.float32) * s, 'bw2_b': jnp.zeros((1,), dtype=jnp.float32), 'lin_w': jax.random.normal(ks[7], (C, C, 3, 3), dtype=jnp.float32) * s, 'lin_b': jnp.zeros((C,), dtype=jnp.float32)}
        return inp
    _L0_conv_all = _L0_conv_setup()
    _L0_conv_in = {k: v for k, v in _L0_conv_all.items() if k in ('q_w', 'q_b', 'v_w', 'v_b', 'lw1_w', 'lw1_b', 'lw2_w', 'lw2_b', 'bw1_w', 'bw1_b', 'bw2_w', 'bw2_b', 'lin_w', 'lin_b', )}
    del _L0_conv_all

    def _L1_conv_setup():
        import jax, jax.numpy as jnp
        import numpy as np
        C = 128
        N = 64
        DT_R = 8
        K = 3
        B_, H_, W_ = (2, 64, 64)
        EPS = 1e-05

        def _scan_comb(e1, e2):
            a1, b1 = e1
            a2, b2 = e2
            return (a1 * a2, a2 * b1 + b2)
        key = jax.random.key(seed)
        ks = jax.random.split(key, 8)
        s = 0.02
        inp = {'x': jax.random.normal(ks[0], (B_, C, H_, W_), jnp.float32), 'W_in': jax.random.normal(ks[1], (C, 2 * C), jnp.float32) * s, 'K_conv': jax.random.normal(ks[2], (C, 1, K, K), jnp.float32) * s, 'b_conv': jnp.zeros((C,), jnp.float32), 'gamma': jnp.ones((C,), jnp.float32), 'beta': jnp.zeros((C,), jnp.float32), 'W_dt': jax.random.normal(ks[3], (C, DT_R + 2 * N), jnp.float32) * s, 'b_dt': jnp.zeros((DT_R + 2 * N,), jnp.float32), 'W_dtr': jax.random.normal(ks[4], (DT_R, C), jnp.float32) * s, 'b_dtr': jnp.zeros((C,), jnp.float32), 'A_log': jnp.tile(jnp.log(jnp.arange(1, N + 1, dtype=jnp.float32))[None, :], (C, 1)), 'D_param': jnp.ones((C,), jnp.float32), 'W_out': jax.random.normal(ks[5], (C, C), jnp.float32) * s}
        return inp
    _L1_conv_all = _L1_conv_setup()
    _L1_conv_in = {k: v for k, v in _L1_conv_all.items() if k in ('W_in', 'K_conv', 'b_conv', 'gamma', 'beta', 'W_dt', 'b_dt', 'W_dtr', 'b_dtr', 'A_log', 'D_param', 'W_out', )}
    del _L1_conv_all

    def _L2_conv_setup():
        import jax, jax.numpy as jnp
        import numpy as np
        B, C, H, W = (4, 128, 64, 64)
        key = jax.random.key(seed)
        ks = jax.random.split(key, 4)
        x = jax.random.normal(ks[0], (B, C, H, W), dtype=jnp.float32)
        Wf = jax.random.normal(ks[1], (1, C), dtype=jnp.float32) * 0.02
        bf = jnp.zeros((1,), dtype=jnp.float32)
        Wg = jax.random.normal(ks[2], (1, C), dtype=jnp.float32) * 0.02
        bg = jnp.zeros((1,), dtype=jnp.float32)
        Wh = jax.random.normal(ks[3], (C, C), dtype=jnp.float32) * 0.02
        bh = jnp.zeros((C,), dtype=jnp.float32)
        return {'x': x, 'Wf': Wf, 'bf': bf, 'Wg': Wg, 'bg': bg, 'Wh': Wh, 'bh': bh}
    _L2_conv_all = _L2_conv_setup()
    _L2_conv_in = {k: v for k, v in _L2_conv_all.items() if k in ('Wf', 'bf', 'Wg', 'bg', 'Wh', 'bh', )}
    del _L2_conv_all

    def _L3_conv_setup():
        import jax, jax.numpy as jnp
        import numpy as np
        D_MODEL = 128
        D_INNER = 256
        D_STATE = 16
        D_CONV = 4
        DT_RANK = 8
        GROUPS = 4

        def _mamba(xf, Win, conv_w, conv_b, Wx, Wdt, bdt, A_log, D, Wout):
            d_inner = conv_w.shape[0]
            d_state = A_log.shape[1]
            xz = jnp.einsum('blc,ec->ble', xf, Win)
            u, z = jnp.split(xz, 2, axis=-1)
            uT = jnp.swapaxes(u, 1, 2)
            conv = jax.lax.conv_general_dilated(uT, conv_w, window_strides=(1,), padding=[(D_CONV - 1, 0)], feature_group_count=d_inner, dimension_numbers=('NCH', 'OIH', 'NCH'))
            u = jax.nn.silu(jnp.swapaxes(conv, 1, 2) + conv_b)
            x_dbl = jnp.einsum('bld,ed->ble', u, Wx)
            dt = x_dbl[..., :DT_RANK]
            Bm = x_dbl[..., DT_RANK:DT_RANK + d_state]
            Cm = x_dbl[..., DT_RANK + d_state:]
            delta = jax.nn.softplus(jnp.einsum('blr,dr->bld', dt, Wdt) + bdt)
            A = -jnp.exp(A_log)
            dA = jnp.exp(jnp.einsum('bld,dn->bldn', delta, A))
            dBu = jnp.einsum('bld,bln,bld->bldn', delta, Bm, u)

            def step(h, inp):
                dA_l, dBu_l, C_l = inp
                h = dA_l * h + dBu_l
                y = jnp.einsum('bdn,bn->bd', h, C_l)
                return (h, y)
            h0 = jnp.zeros((1, d_inner, d_state), dtype=u.dtype)
            _, ys = jax.lax.scan(step, h0, (jnp.swapaxes(dA, 0, 1), jnp.swapaxes(dBu, 0, 1), jnp.swapaxes(Cm, 0, 1)))
            y = jnp.swapaxes(ys, 0, 1)
            y = y + u * D
            y = y * jax.nn.silu(z)
            return jnp.einsum('bld,od->blo', y, Wout)
        key = jax.random.key(seed)
        ks = jax.random.split(key, 8)
        x = jax.random.normal(ks[0], (2, D_MODEL, 64, 64), dtype=jnp.float32)
        Win = jax.random.normal(ks[1], (2 * D_INNER, D_MODEL), dtype=jnp.float32) * D_MODEL ** (-0.5)
        conv_w = jax.random.normal(ks[2], (D_INNER, 1, D_CONV), dtype=jnp.float32) * 0.2
        conv_b = jnp.zeros((D_INNER,), dtype=jnp.float32)
        Wx = jax.random.normal(ks[3], (DT_RANK + 2 * D_STATE, D_INNER), dtype=jnp.float32) * D_INNER ** (-0.5)
        Wdt = jax.random.normal(ks[4], (D_INNER, DT_RANK), dtype=jnp.float32) * DT_RANK ** (-0.5)
        bdt = jnp.full((D_INNER,), -4.6, dtype=jnp.float32) + 0.1 * jax.random.normal(ks[5], (D_INNER,), dtype=jnp.float32)
        A_log = jnp.log(jnp.broadcast_to(jnp.arange(1, D_STATE + 1, dtype=jnp.float32), (D_INNER, D_STATE)))
        D = jnp.ones((D_INNER,), dtype=jnp.float32)
        Wout = jax.random.normal(ks[6], (D_MODEL, D_INNER), dtype=jnp.float32) * D_INNER ** (-0.5)
        gn_w = jnp.ones((D_MODEL,), dtype=jnp.float32)
        gn_b = jnp.zeros((D_MODEL,), dtype=jnp.float32)
        return {'x': x, 'Win': Win, 'conv_w': conv_w, 'conv_b': conv_b, 'Wx': Wx, 'Wdt': Wdt, 'bdt': bdt, 'A_log': A_log, 'D': D, 'Wout': Wout, 'gn_w': gn_w, 'gn_b': gn_b}
    _L3_conv_all = _L3_conv_setup()
    _L3_conv_in = {k: v for k, v in _L3_conv_all.items() if k in ('Win', 'conv_w', 'conv_b', 'Wx', 'Wdt', 'bdt', 'A_log', 'D', 'Wout', 'gn_w', 'gn_b', )}
    del _L3_conv_all

    return {
        "x": x,
        "L0_conv_q_w": _L0_conv_in["q_w"],
        "L0_conv_q_b": _L0_conv_in["q_b"],
        "L0_conv_v_w": _L0_conv_in["v_w"],
        "L0_conv_v_b": _L0_conv_in["v_b"],
        "L0_conv_lw1_w": _L0_conv_in["lw1_w"],
        "L0_conv_lw1_b": _L0_conv_in["lw1_b"],
        "L0_conv_lw2_w": _L0_conv_in["lw2_w"],
        "L0_conv_lw2_b": _L0_conv_in["lw2_b"],
        "L0_conv_bw1_w": _L0_conv_in["bw1_w"],
        "L0_conv_bw1_b": _L0_conv_in["bw1_b"],
        "L0_conv_bw2_w": _L0_conv_in["bw2_w"],
        "L0_conv_bw2_b": _L0_conv_in["bw2_b"],
        "L0_conv_lin_w": _L0_conv_in["lin_w"],
        "L0_conv_lin_b": _L0_conv_in["lin_b"],
        "L1_conv_W_in": _L1_conv_in["W_in"],
        "L1_conv_K_conv": _L1_conv_in["K_conv"],
        "L1_conv_b_conv": _L1_conv_in["b_conv"],
        "L1_conv_gamma": _L1_conv_in["gamma"],
        "L1_conv_beta": _L1_conv_in["beta"],
        "L1_conv_W_dt": _L1_conv_in["W_dt"],
        "L1_conv_b_dt": _L1_conv_in["b_dt"],
        "L1_conv_W_dtr": _L1_conv_in["W_dtr"],
        "L1_conv_b_dtr": _L1_conv_in["b_dtr"],
        "L1_conv_A_log": _L1_conv_in["A_log"],
        "L1_conv_D_param": _L1_conv_in["D_param"],
        "L1_conv_W_out": _L1_conv_in["W_out"],
        "L2_conv_Wf": _L2_conv_in["Wf"],
        "L2_conv_bf": _L2_conv_in["bf"],
        "L2_conv_Wg": _L2_conv_in["Wg"],
        "L2_conv_bg": _L2_conv_in["bg"],
        "L2_conv_Wh": _L2_conv_in["Wh"],
        "L2_conv_bh": _L2_conv_in["bh"],
        "L3_conv_Win": _L3_conv_in["Win"],
        "L3_conv_conv_w": _L3_conv_in["conv_w"],
        "L3_conv_conv_b": _L3_conv_in["conv_b"],
        "L3_conv_Wx": _L3_conv_in["Wx"],
        "L3_conv_Wdt": _L3_conv_in["Wdt"],
        "L3_conv_bdt": _L3_conv_in["bdt"],
        "L3_conv_A_log": _L3_conv_in["A_log"],
        "L3_conv_D": _L3_conv_in["D"],
        "L3_conv_Wout": _L3_conv_in["Wout"],
        "L3_conv_gn_w": _L3_conv_in["gn_w"],
        "L3_conv_gn_b": _L3_conv_in["gn_b"],
    }

def reference(x, L0_conv_q_w, L0_conv_q_b, L0_conv_v_w, L0_conv_v_b, L0_conv_lw1_w, L0_conv_lw1_b, L0_conv_lw2_w, L0_conv_lw2_b, L0_conv_bw1_w, L0_conv_bw1_b, L0_conv_bw2_w, L0_conv_bw2_b, L0_conv_lin_w, L0_conv_lin_b, L1_conv_W_in, L1_conv_K_conv, L1_conv_b_conv, L1_conv_gamma, L1_conv_beta, L1_conv_W_dt, L1_conv_b_dt, L1_conv_W_dtr, L1_conv_b_dtr, L1_conv_A_log, L1_conv_D_param, L1_conv_W_out, L2_conv_Wf, L2_conv_bf, L2_conv_Wg, L2_conv_bg, L2_conv_Wh, L2_conv_bh, L3_conv_Win, L3_conv_conv_w, L3_conv_conv_b, L3_conv_Wx, L3_conv_Wdt, L3_conv_bdt, L3_conv_A_log, L3_conv_D, L3_conv_Wout, L3_conv_gn_w, L3_conv_gn_b):
    import jax
    import jax.numpy as jnp
    def _L0_conv_ref(x, q_w, q_b, v_w, v_b, lw1_w, lw1_b, lw2_w, lw2_b, bw1_w, bw1_b, bw2_w, bw2_b, lin_w, lin_b):
        import jax, jax.numpy as jnp
        import numpy as np
        C = 128
        MID = C // 4
        H = W = 64
        B = 4
        SOFTMAX_SCALE = 1.0

        def _leaky(z):
            return jnp.where(z >= 0, z, 0.2 * z)

        def _conv1x1(x, w, b):
            return jnp.einsum('oc,bchw->bohw', w, x) + b[None, :, None, None]

        def _attn_sample(q_map, v_map, w_map, b_map):
            n = H * W
            q = q_map.reshape(C, n)
            v = v_map.reshape(C, n)
            w = w_map.reshape(n)
            b = b_map.reshape(n)
            norm = jnp.sqrt(jnp.sum(q * q, axis=0))
            k = q / jnp.clip(norm, 0.0001)[None, :]
            logits = jnp.einsum('cn,cm->nm', k, q)
            mean = jnp.mean(logits, axis=0, keepdims=True)
            sparse = jax.nn.relu(logits - mean * w[None, :] + b[None, :])
            mask = (sparse != 0.0).astype(logits.dtype)
            attn = jax.nn.softmax(logits * sparse * SOFTMAX_SCALE, axis=0)
            attn = jnp.clip(attn * mask, 1e-08)
            out = jnp.einsum('cn,nm->cm', v, attn)
            return out.reshape(C, H, W)
        x1 = _conv1x1(x, v_w, v_b)
        x2 = _conv1x1(x, q_w, q_b)
        weight = _conv1x1(_leaky(_conv1x1(x2, lw1_w, lw1_b)), lw2_w, lw2_b)
        bias = _conv1x1(_leaky(_conv1x1(x2, bw1_w, bw1_b)), bw2_w, bw2_b)
        y = jax.vmap(_attn_sample)(x2, x1, weight, bias)
        y = jax.lax.conv_general_dilated(y, lin_w, window_strides=(1, 1), padding='SAME', dimension_numbers=('NCHW', 'OIHW', 'NCHW'))
        y = _leaky(y + lin_b[None, :, None, None])
        return y + x

    def _L1_conv_ref(x, W_in, K_conv, b_conv, gamma, beta, W_dt, b_dt, W_dtr, b_dtr, A_log, D_param, W_out):
        import jax, jax.numpy as jnp
        import numpy as np
        C = 128
        N = 64
        DT_R = 8
        K = 3
        B_, H_, W_ = (2, 64, 64)
        EPS = 1e-05

        def _scan_comb(e1, e2):
            a1, b1 = e1
            a2, b2 = e2
            return (a1 * a2, a2 * b1 + b2)
        Bb, Cc, Hh, Ww = x.shape
        L = Hh * Ww
        r = W_dtr.shape[0]
        n = A_log.shape[1]
        xp = jnp.transpose(x, (0, 2, 3, 1))
        xproj = xp @ W_in
        x_mamba, x_conv = jnp.split(xproj, 2, axis=-1)
        xc = jnp.transpose(x_conv, (0, 3, 1, 2))
        xc = jax.lax.conv_general_dilated(xc, K_conv, window_strides=(1, 1), padding=[(1, 1), (1, 1)], feature_group_count=Cc, dimension_numbers=('NCHW', 'OIHW', 'NCHW')) + b_conv[None, :, None, None]
        xc = jnp.transpose(xc, (0, 2, 3, 1))
        xc = xc * jax.nn.silu(xc)
        u0 = x_mamba.reshape(Bb, L, Cc)
        mu = jnp.mean(u0, axis=-1, keepdims=True)
        var = jnp.mean(jnp.square(u0 - mu), axis=-1, keepdims=True)
        u = (u0 - mu) * jax.lax.rsqrt(var + EPS) * gamma + beta
        A = -jnp.exp(A_log)
        dtbc = u @ W_dt + b_dt
        dt_raw = dtbc[..., :r]
        B_ssm = dtbc[..., r:r + n]
        C_ssm = dtbc[..., r + n:]
        delta = jax.nn.softplus(dt_raw @ W_dtr + b_dtr)
        deltaA = jnp.exp(delta[..., None] * A[None, None])
        dBu = delta[..., None] * B_ssm[:, :, None, :] * u[..., None]
        _, h = jax.lax.associative_scan(_scan_comb, (deltaA, dBu), axis=1)
        y = jnp.einsum('bldn,bln->bld', h, C_ssm) + u * D_param
        y = y.reshape(Bb, Hh, Ww, Cc) + xc
        out = y @ W_out
        out = jnp.transpose(out, (0, 3, 1, 2))
        return x + out

    def _L2_conv_ref(x, Wf, bf, Wg, bg, Wh, bh):
        import jax, jax.numpy as jnp
        import numpy as np
        B, C, H, W = (4, 128, 64, 64)
        b, c, h_, w_ = x.shape
        n = h_ * w_
        xf = x.reshape(b, c, n)
        f = jnp.einsum('oc,bcn->bon', Wf, xf) + bf[None, :, None]
        g = jnp.einsum('oc,bcn->bon', Wg, xf) + bg[None, :, None]
        hh = jnp.einsum('oc,bcn->bon', Wh, xf) + bh[None, :, None]
        logits = jnp.einsum('bdi,bdj->bij', f, g)
        attn = jax.nn.softmax(logits, axis=-1)
        sa = jnp.einsum('bcj,bji->bci', hh, attn)
        return sa.reshape(b, c, h_, w_) + x

    def _L3_conv_ref(x, Win, conv_w, conv_b, Wx, Wdt, bdt, A_log, D, Wout, gn_w, gn_b):
        import jax, jax.numpy as jnp
        import numpy as np
        D_MODEL = 128
        D_INNER = 256
        D_STATE = 16
        D_CONV = 4
        DT_RANK = 8
        GROUPS = 4

        def _mamba(xf, Win, conv_w, conv_b, Wx, Wdt, bdt, A_log, D, Wout):
            d_inner = conv_w.shape[0]
            d_state = A_log.shape[1]
            xz = jnp.einsum('blc,ec->ble', xf, Win)
            u, z = jnp.split(xz, 2, axis=-1)
            uT = jnp.swapaxes(u, 1, 2)
            conv = jax.lax.conv_general_dilated(uT, conv_w, window_strides=(1,), padding=[(D_CONV - 1, 0)], feature_group_count=d_inner, dimension_numbers=('NCH', 'OIH', 'NCH'))
            u = jax.nn.silu(jnp.swapaxes(conv, 1, 2) + conv_b)
            x_dbl = jnp.einsum('bld,ed->ble', u, Wx)
            dt = x_dbl[..., :DT_RANK]
            Bm = x_dbl[..., DT_RANK:DT_RANK + d_state]
            Cm = x_dbl[..., DT_RANK + d_state:]
            delta = jax.nn.softplus(jnp.einsum('blr,dr->bld', dt, Wdt) + bdt)
            A = -jnp.exp(A_log)
            dA = jnp.exp(jnp.einsum('bld,dn->bldn', delta, A))
            dBu = jnp.einsum('bld,bln,bld->bldn', delta, Bm, u)

            def step(h, inp):
                dA_l, dBu_l, C_l = inp
                h = dA_l * h + dBu_l
                y = jnp.einsum('bdn,bn->bd', h, C_l)
                return (h, y)
            h0 = jnp.zeros((1, d_inner, d_state), dtype=u.dtype)
            _, ys = jax.lax.scan(step, h0, (jnp.swapaxes(dA, 0, 1), jnp.swapaxes(dBu, 0, 1), jnp.swapaxes(Cm, 0, 1)))
            y = jnp.swapaxes(ys, 0, 1)
            y = y + u * D
            y = y * jax.nn.silu(z)
            return jnp.einsum('bld,od->blo', y, Wout)
        B, C, H, W = x.shape
        x_flat = jnp.transpose(x, (0, 2, 3, 1)).reshape(1, -1, C)
        args = (Win, conv_w, conv_b, Wx, Wdt, bdt, A_log, D, Wout)
        y_fwd = _mamba(x_flat, *args)
        y_bwd = jnp.flip(_mamba(jnp.flip(x_flat, axis=1), *args), axis=1)
        x_recon = (y_fwd + y_bwd).reshape(B, H, W, C)
        x_recon = jnp.transpose(x_recon, (0, 3, 1, 2))
        xg = x_recon.reshape(B, GROUPS, C // GROUPS, H, W)
        mu = xg.mean(axis=(2, 3, 4), keepdims=True)
        var = xg.var(axis=(2, 3, 4), keepdims=True)
        xn = ((xg - mu) * jax.lax.rsqrt(var + 1e-05)).reshape(B, C, H, W)
        xn = xn * gn_w[:, None, None] + gn_b[:, None, None]
        return jax.nn.silu(xn) + x

    def _gn(v, G=32, eps=1e-5):
        B_, C_, H_, W_ = v.shape
        g = v.reshape(B_, G, C_ // G, H_, W_)
        m = jnp.mean(g, axis=(2, 3, 4), keepdims=True)
        s = jnp.var(g, axis=(2, 3, 4), keepdims=True)
        return ((g - m) / jnp.sqrt(s + eps)).reshape(v.shape)

    def _ln_c(v, eps=1e-6):
        m = jnp.mean(v, axis=1, keepdims=True)
        s = jnp.var(v, axis=1, keepdims=True)
        return (v - m) / jnp.sqrt(s + eps)

    def _ln_t(v, eps=1e-5):
        m = jnp.mean(v, axis=-1, keepdims=True)
        s = jnp.var(v, axis=-1, keepdims=True)
        return (v - m) / jnp.sqrt(s + eps)

    def _to_tokens(v):
        B_, C_, H_, W_ = v.shape
        return v.reshape(B_, C_, H_ * W_).transpose(0, 2, 1)
    def _from_tokens(t, like):
        B_, C_, H_, W_ = like.shape
        return t.transpose(0, 2, 1).reshape(B_, C_, H_, W_)

    x = _L0_conv_ref(x, L0_conv_q_w, L0_conv_q_b, L0_conv_v_w, L0_conv_v_b, L0_conv_lw1_w, L0_conv_lw1_b, L0_conv_lw2_w, L0_conv_lw2_b, L0_conv_bw1_w, L0_conv_bw1_b, L0_conv_bw2_w, L0_conv_bw2_b, L0_conv_lin_w, L0_conv_lin_b)
    x = _L1_conv_ref(x, L1_conv_W_in, L1_conv_K_conv, L1_conv_b_conv, L1_conv_gamma, L1_conv_beta, L1_conv_W_dt, L1_conv_b_dt, L1_conv_W_dtr, L1_conv_b_dtr, L1_conv_A_log, L1_conv_D_param, L1_conv_W_out)
    x = _L2_conv_ref(x, L2_conv_Wf, L2_conv_bf, L2_conv_Wg, L2_conv_bg, L2_conv_Wh, L2_conv_bh)
    x = _L3_conv_ref(x, L3_conv_Win, L3_conv_conv_w, L3_conv_conv_b, L3_conv_Wx, L3_conv_Wdt, L3_conv_bdt, L3_conv_A_log, L3_conv_D, L3_conv_Wout, L3_conv_gn_w, L3_conv_gn_b)
    return x


_drawn_inputs = setup_inputs


def setup_inputs(seed=0):
    import zlib

    import numpy as np

    out = dict(_drawn_inputs(seed))
    spreads = {'L0_conv_q_b': (0.0, 0.8),
     'L0_conv_v_b': (0.0, 0.1),
     'L0_conv_lw1_b': (0.0, 0.8),
     'L0_conv_bw1_b': (0.0, 0.8),
     'L0_conv_lin_b': (0.0, 0.1),
     'L1_conv_b_conv': (0.0, 0.8),
     'L1_conv_gamma': (1.0, 0.2),
     'L1_conv_beta': (0.0, 0.39),
     'L1_conv_b_dt': (0.0, 0.1),
     'L1_conv_b_dtr': (0.0, 0.8),
     'L1_conv_D_param': (1.0, 0.2),
     'L2_conv_bh': (0.0, 0.1),
     'L3_conv_conv_b': (0.0, 0.1),
     'L3_conv_D': (1.0, 0.2),
     'L3_conv_gn_w': (1.0, 0.2),
     'L3_conv_gn_b': (0.0, 0.1)}
    factors = {'L0_conv_q_w': 8.0,
     'L0_conv_lw1_w': 8.0,
     'L0_conv_lw2_w': 8.0,
     'L0_conv_bw1_w': 8.0,
     'L0_conv_bw2_w': 8.0,
     'L1_conv_K_conv': 8.0,
     'L1_conv_W_dtr': 8.0,
     'L1_conv_A_log': 7.319,
     'L2_conv_Wf': 8.0,
     'L2_conv_Wg': 8.0,
     'L3_conv_Wx': 8.0,
     'L3_conv_Wdt': 8.0,
     'L3_conv_bdt': 8.0,
     'L3_conv_A_log': 4.27}
    for name, (base, spread) in spreads.items():
        noise = np.random.default_rng([zlib.crc32(name.encode()), seed]).standard_normal(out[name].shape)
        drawn = base * np.exp(spread * noise) if base else spread * noise
        out[name] = jnp.asarray(drawn.astype(out[name].dtype))
    for name, factor in factors.items():
        out[name] = (out[name] * factor).astype(out[name].dtype)
    return out
```

```python
from contextlib import ExitStack

import numpy as _np
import concourse.bass as bass
from concourse import mybir

F32 = mybir.dt.float32
BF16 = mybir.dt.bfloat16
ALU = mybir.AluOpType
ACT = mybir.ActivationFunctionType
AX = mybir.AxisListType

B, C, H, W = 4, 128, 64, 64
N = H * W
T = N // 128
BANK = 512
NB = N // BANK
ds = bass.ds


def columns(widths):
    at, out = 0, {}
    for name, width in widths:
        out[name] = slice(at, at + width)
        at += width
    return out, at


MID = C // 4
L0_WEIGHTS = [("q_w", C), ("v_w", C), ("branch_w1", 2 * MID), ("branch_w2", 2), ("lin_w", 9 * C), ("v_b", C),
              ("q_b", 1), ("branch_b1", 1), ("branch_b2", 2), ("lin_b", 1), ("ident", C), ("ones", C)]
L0_AT, L0_WIDTH = columns(L0_WEIGHTS)


def sparse_attention_layer(nc, x, weights):
    CH = 1024
    NC = N // CH
    G = N // BANK
    AV_CREDIT = 2 + G
    ctx = ExitStack()
    with ctx:
        sb = lambda name, shape, dt=F32: ctx.enter_context(nc.sbuf_tensor("l0_" + name, shape, dt))
        sem = lambda name: ctx.enter_context(nc.semaphore("l0_" + name))
        w = sb("w", [128, L0_WIDTH])
        wt = lambda name: w[:, L0_AT[name]]
        ident, ones = wt("ident"), wt("ones")
        q = sb("q", [128, N])
        k = sb("k", [128, N])
        vT = sb("vT", [128, N])
        E = sb("E", [128, 2, N])
        xb, qsq, hid = E[:, 0, :], E[:, 1, :], E[0:2 * MID, 0, :]
        relu = sb("relu", [128, 2, CH])
        attnT = sb("attnT", [128, 2, BANK])
        y = sb("y", [128, H + 2, W + 2])
        qm = sb("qm", [128, 2, 128])
        sumsq = sb("sumsq", [128, T])
        root = sb("root", [128, T])
        rinv = sb("rinv", [128, T])
        tmp = sb("tmp", [128, T])
        qnorm = sb("qnorm", [128, T])
        wb = sb("wb", [128, 2 * T])
        params = sb("params", [128, T, 2])
        neg_t, neg_max = params[:, :, 0], params[:, :, 1]
        offsets = sb("offsets", [128, 2, 2])
        kpart = sb("kpart", [128, NB])
        kbar = sb("kbar", [128, 1])
        zpart = sb("zpart", [128, 2, NC])
        zsum = sb("zsum", [128, 2])
        zinv = sb("zinv", [128, 2])
        lin = sb("lin", [128, 2, BANK])
        ps = ctx.enter_context(nc.psum_tensor("l0_ps", [128, 8, BANK], F32))
        logits = [ps[:, 0:2, :].rearrange("p a b -> p (a b)"), ps[:, 2:4, :].rearrange("p a b -> p (a b)")]

        weights_in = sem("weights_in")
        banks_free = sem("banks_free")
        x_copied = sem("x_copied")
        q_mm = sem("q_mm"); q_out = sem("q_out"); q_squared = sem("q_squared")
        v_mm = sem("v_mm"); v_out = sem("v_out")
        hid_mm = sem("hid_mm"); hid_out = sem("hid_out"); hid_leaky = sem("hid_leaky")
        stats_mm = sem("stats_mm"); ss_ready = sem("ss_ready"); root_ready = sem("root_ready")
        rinv_ready = sem("rinv_ready"); rinv_mm = sem("rinv_mm"); k_out = sem("k_out")
        kbar_ready = sem("kbar_ready"); mean_mm = sem("mean_mm"); params_ready = sem("params_ready")
        qm_ready = sem("qm_ready"); logits_mm = sem("logits_mm"); relu_ready = sem("relu_ready")
        s_ready = sem("s_ready"); exp_ready = sem("exp_ready"); mask_done = sem("mask_done")
        clip_done = sem("clip_done")
        even_mm = sem("even_mm"); odd_mm = sem("odd_mm"); even_out = sem("even_out"); odd_out = sem("odd_out")
        av_mm = sem("av_mm"); o_out = sem("o_out")
        conv_mm = sem("conv_mm"); lin_out = sem("lin_out"); residual_done = sem("residual_done"); border_zero = sem("border_zero")

        block = ctx.enter_context(nc.Block())

        @block.sync
        def _(sp):
            sp.dma_start(w[:], weights).then_inc(weights_in, 16)

        @block.gpsimd
        def _(pool):
            with pool.Fori(0, B) as b:
                with pool.Fori(0, T // 2) as i:
                    for h in range(2):
                        pool.wait_ge(q_out, b * NB + NB)
                        pool.wait_ge(logits_mm, (b * T + i * 2 + h) * NC + NC)
                        nc.gpsimd.tensor_copy(qm[:, h, :], q[:, ds(i * 256 + h * 128, 128)]).then_inc(qm_ready, 1)

        @block.tensor
        def _(pe):
            pe.sem_inc(logits_mm, 2 * NC)
            pe.sem_inc(av_mm, AV_CREDIT)
            pe.wait_ge(weights_in, 16)
            with pe.Fori(0, B) as b:
                pe.wait_ge(banks_free, b + 1)
                for j in range(NB):
                    nc.tensor.matmul(ps[:, j, :], wt("q_w"), x[:, ds(b * N + j * BANK, BANK)], start=True,
                                     stop=True).then_inc(q_mm, 1)
                pe.wait_ge(x_copied, b + 1)
                for t in range(T):
                    if t % 4 == 0:
                        pe.wait_ge(q_out, b * NB + t // 4 + 1)
                    ins = nc.tensor.matmul(ps[:, t // 4, (t % 4) * 128:(t % 4 + 1) * 128],
                                           xb[:, t * 128:(t + 1) * 128], wt("v_w"), start=True, stop=True)
                    if t % 4 == 3:
                        ins.then_inc(v_mm, 1)
                for j in range(NB):
                    pe.wait_ge(v_out, b * NB + j + 1)
                    nc.tensor.matmul(ps[0:2 * MID, j, :], wt("branch_w1"), q[:, j * BANK:(j + 1) * BANK],
                                     start=True, stop=True).then_inc(hid_mm, 1)
                pe.wait_ge(hid_out, b * NB + NB)
                pe.wait_ge(q_squared, b + 1)
                for t in range(T):
                    nc.tensor.matmul(ps[:, 0, t:t + 1], qsq[:, t * 128:(t + 1) * 128], ones[:, 0:1], start=True,
                                     stop=True)
                pe.wait_ge(hid_leaky, b + 1)
                for t in range(T):
                    ins = nc.tensor.matmul(ps[:, 1, 2 * t:2 * t + 2], hid[:, t * 128:(t + 1) * 128],
                                           w[0:2 * MID, L0_AT["branch_w2"]], start=True, stop=True)
                ins.then_inc(stats_mm, 1)
                pe.wait_ge(rinv_ready, b + 1)
                for t in range(T):
                    ins = nc.tensor.matmul(ps[:, t // 4, (t % 4) * 128:(t % 4 + 1) * 128],
                                           rinv[:, t:t + 1].broadcast_to([128, 128]), ident, start=True, stop=True)
                    if t % 4 == 3:
                        ins.then_inc(rinv_mm, 1)
                pe.wait_ge(kbar_ready, b + 1)
                for t in range(T):
                    ins = nc.tensor.matmul(ps[:, 0, t:t + 1], q[:, t * 128:(t + 1) * 128], kbar[:, 0:1], start=True,
                                           stop=True)
                ins.then_inc(mean_mm, 1)
                pe.wait_ge(params_ready, b + 1)

                def step(new, old, h):
                    def logit(c):
                        if c == 0:
                            pe.wait_ge(qm_ready, b * T + new + 1)
                        pe.wait_ge(s_ready, (b * T + new) * NC + c + 1)
                        for j in range(2):
                            ins = nc.tensor.matmul(logits[c % 2][:, j * BANK:(j + 1) * BANK], qm[:, h, :],
                                                   k[:, c * CH + j * BANK:c * CH + (j + 1) * BANK], start=True,
                                                   stop=True)
                        ins.then_inc(logits_mm, 1)

                    def transpose(g):
                        if g == 0:
                            pe.wait_ge(clip_done, b * T + old + 1)
                        pe.wait_ge([even_out, odd_out][g % 2], (b * T + old) * (G // 2) + g // 2 + 1)
                        for j in range(4):
                            at = (4 * g + j) * 128
                            ins = nc.tensor.transpose(ps[:, 4 + g % 2, j * 128:(j + 1) * 128],
                                                      E[:, 1 - h, at:at + 128], ident)
                        ins.then_inc([even_mm, odd_mm][g % 2], 1)

                    def product(g):
                        if g == 0:
                            pe.wait_ge(o_out, b * T + old + 1)
                        pe.wait_ge([even_out, odd_out][g % 2], (b * T + old) * (G // 2) + g // 2 + 2)
                        for j in range(4):
                            t = 4 * g + j
                            ins = nc.tensor.matmul(ps[:, 7 - h, 0:128], vT[:, t * 128:(t + 1) * 128],
                                                   attnT[:, g % 2, j * 128:(j + 1) * 128], start=t == 0,
                                                   stop=t == T - 1)
                        ins.then_inc(av_mm, 1)

                    for c in range(NC):
                        if new is not None:
                            logit(c)
                        if old is not None:
                            for g in [[], [0, 1, 2], [3, 4, 5], [6, 7]][c]:
                                transpose(g)
                                if g:
                                    product(g - 1)
                    if old is not None:
                        product(G - 1)

                step(0, None, 0)
                with pe.Fori(0, T // 2 - 1) as i:
                    step(i * 2 + 1, i * 2, 1)
                    step(i * 2 + 2, i * 2 + 1, 0)
                step(T - 1, T - 2, 1)
                step(None, T - 1, 0)
                pe.wait_ge(o_out, b * T + T + 2)
                for j in range(NB):
                    for tap in range(9):
                        dy, dx = tap // 3, tap % 3
                        at = L0_AT["lin_w"].start + tap * C
                        ins = nc.tensor.matmul(ps[:, j, :], w[:, at:at + C], y[:, 8 * j + dy:8 * j + dy + 8, dx:dx + W],
                                               start=tap == 0, stop=tap == 8)
                    ins.then_inc(conv_mm, 1)

        @block.scalar
        def _(act):
            act.sem_inc(even_out, 1)
            act.sem_inc(o_out, 2)
            act.wait_ge(weights_in, 16)
            act.wait_ge(border_zero, 1)
            with act.Fori(0, B) as b:
                for j in range(NB):
                    act.wait_ge(q_mm, b * NB + j + 1)
                    nc.scalar.activation(q[:, j * BANK:(j + 1) * BANK], ps[:, j, :], ACT.Identity,
                                         bias=wt("q_b")).then_inc(q_out, 1)
                for j in range(NB):
                    act.wait_ge(hid_mm, b * NB + j + 1)
                    nc.scalar.activation(hid[:, j * BANK:(j + 1) * BANK], ps[0:2 * MID, j, :], ACT.Identity,
                                         bias=w[0:2 * MID, L0_AT["branch_b1"]]).then_inc(hid_out, 1)
                act.wait_ge(ss_ready, b + 1)
                nc.scalar.activation(root[:], sumsq[:], ACT.Sqrt).then_inc(root_ready, 1)
                act.drain()
                act.wait_ge(params_ready, b + 1)

                def step(new, old, h):
                    def relus(c):
                        act.wait_ge(logits_mm, (b * T + new) * NC + 2 * NC + c + 1)
                        act.wait_ge(mask_done, (b * T + new) * NC + c + 1)
                        nc.scalar.activation(relu[:, c % 2, :], logits[c % 2], ACT.Relu,
                                             bias=offsets[:, h, 0:1]).then_inc(relu_ready, 1)

                    def exps(c):
                        act.wait_ge(s_ready, (b * T + new) * NC + c + 3)
                        part = E[:, h, c * CH:(c + 1) * CH]
                        nc.scalar.activation(part, part, ACT.Exp, bias=offsets[:, h, 1:2],
                                             accum_out=zpart[:, h, c:c + 1]).then_inc(exp_ready, 1)

                    def copy(g):
                        act.wait_ge(even_mm, (b * T + old) * (G // 2) + g // 2 + 1)
                        act.wait_ge(av_mm, (b * T + old) * G + g - 1 + AV_CREDIT)
                        nc.scalar.activation(attnT[:, 0, :], ps[:, 4, :], ACT.Copy).then_inc(even_out, 1)

                    if new is not None:
                        if old is not None:
                            act.drain()
                        nc.scalar.activation(offsets[:, h, :], params[:, ds(new, 1), :].rearrange("p a b -> p (a b)"),
                                             ACT.Copy)
                        act.drain()
                    for c in range(NC):
                        if new is not None:
                            relus(c)
                        if old is not None and c == 1:
                            copy(0)
                        if new is not None:
                            exps(c)
                        if old is not None and c:
                            copy(2 * c)
                    if old is not None:
                        act.wait_ge(av_mm, (b * T + old) * G + G + AV_CREDIT)
                        nc.scalar.activation(y[:, ds(old * 2 + 1, 2), 1:W + 1],
                                             ps[:, 7 - h, 0:128].rearrange("p (a c) -> p a c", a=2),
                                             ACT.Copy).then_inc(o_out, 1)

                step(0, None, 0)
                with act.Fori(0, T // 2 - 1) as i:
                    step(i * 2 + 1, i * 2, 1)
                    step(i * 2 + 2, i * 2 + 1, 0)
                step(T - 1, T - 2, 1)
                step(None, T - 1, 0)
                for j in range(NB):
                    act.wait_ge(conv_mm, b * NB + j + 1)
                    act.wait_ge(residual_done, b * NB + j + 1)
                    nc.scalar.activation(lin[:, j % 2, :], ps[:, j, :], ACT.Identity,
                                         bias=wt("lin_b")).then_inc(lin_out, 1)

        @block.vector
        def _(dve):
            dve.sem_inc(s_ready, 2)
            dve.sem_inc(mask_done, 2)
            dve.sem_inc(odd_out, 1)
            dve.sem_inc(residual_done, 2)
            dve.sem_inc(banks_free, 1)
            nc.vector.memset(y[:], 0.0).then_inc(border_zero, 1)
            dve.wait_ge(weights_in, 16)
            with dve.Fori(0, B) as b:
                nc.vector.tensor_copy(xb, x[:, ds(b * N, N)]).then_inc(x_copied, 1)
                dve.wait_ge(q_out, b * NB + NB)
                nc.vector.tensor_tensor(qsq, q[:], q[:], ALU.mult).then_inc(q_squared, 1)
                for j in range(NB):
                    dve.wait_ge(v_mm, b * NB + j + 1)
                    nc.vector.tensor_tensor(vT[:, j * BANK:(j + 1) * BANK].rearrange("p (a c) -> p a c", a=4),
                                            ps[:, j, :].rearrange("p (a c) -> p a c", a=4),
                                            wt("v_b").unsqueeze(1).broadcast_to([128, 4, 128]),
                                            ALU.add).then_inc(v_out, 1)
                dve.wait_ge(hid_out, b * NB + NB)
                nc.vector.scalar_tensor_tensor(out=hid, in0=hid, scalar=0.2, in1=hid, op0=ALU.mult,
                                               op1=ALU.max).then_inc(hid_leaky, 1)
                dve.wait_ge(stats_mm, b + 1)
                nc.vector.tensor_scalar(sumsq[:], ps[:, 0, 0:T], 1e-8, None, ALU.max).then_inc(ss_ready, 1)
                nc.vector.tensor_copy(wb[:], ps[:, 1, 0:2 * T])
                dve.wait_ge(root_ready, b + 1)
                nc.vector.reciprocal(rinv[:], root[:])
                dve.drain()
                nc.vector.tensor_tensor(tmp[:], sumsq[:], rinv[:], ALU.mult)
                dve.drain()
                nc.vector.tensor_tensor(tmp[:], tmp[:], rinv[:], ALU.mult)
                dve.drain()
                nc.vector.tensor_scalar(tmp[:], tmp[:], -0.5, 1.5, ALU.mult, ALU.add)
                dve.drain()
                nc.vector.tensor_tensor(rinv[:], rinv[:], tmp[:], ALU.mult).then_inc(rinv_ready, 1)
                dve.drain()
                nc.vector.tensor_tensor(qnorm[:], sumsq[:], rinv[:], ALU.mult)
                for j in range(NB):
                    dve.wait_ge(rinv_mm, b * NB + j + 1)
                    nc.vector.scalar_tensor_tensor(out=k[:, j * BANK:(j + 1) * BANK], in0=q[:, j * BANK:(j + 1) * BANK],
                                                   scalar=1.0, in1=ps[:, j, :], op0=ALU.mult, op1=ALU.mult,
                                                   accum_out=kpart[:, j:j + 1])
                dve.drain()
                nc.vector.reduce_sum(kbar[:], kpart[:], axis=AX.X)
                dve.drain()
                nc.vector.tensor_scalar(kbar[:], kbar[:], 1.0 / N, None, ALU.mult).then_inc(kbar_ready, 1)
                nc.vector.tensor_tensor(wb[:].rearrange("p (t a) -> p t a", a=2), wb[:].rearrange("p (t a) -> p t a", a=2),
                                        wt("branch_b2").unsqueeze(1).broadcast_to([128, T, 2]), ALU.add)
                dve.drain()
                dve.wait_ge(mean_mm, b + 1)
                nc.vector.tensor_tensor(tmp[:], wb[:, 0::2], ps[:, 0, 0:T], ALU.mult)
                dve.drain()
                nc.vector.tensor_tensor(neg_t, wb[:, 1::2], tmp[:], ALU.subtract)
                dve.drain()
                nc.vector.tensor_tensor(tmp[:], qnorm[:], neg_t, ALU.add)
                dve.drain()
                nc.vector.tensor_scalar(tmp[:], tmp[:], 0.0, -1.0, ALU.max, ALU.mult)
                dve.drain()
                nc.vector.tensor_tensor(neg_max, tmp[:], qnorm[:], ALU.mult).then_inc(params_ready, 1)

                def step(new, old, h):
                    def exponents(c):
                        if c == 0:
                            dve.wait_ge(av_mm, (b * T + new) * G - G + AV_CREDIT)
                        dve.wait_ge(relu_ready, (b * T + new) * NC + c + 1)
                        nc.vector.tensor_tensor(E[:, h, c * CH:(c + 1) * CH], relu[:, c % 2, :], logits[c % 2],
                                                ALU.mult).then_inc(s_ready, 1)

                    def mask(c):
                        dve.wait_ge(exp_ready, (b * T + new) * NC + c + 1)
                        part = E[:, h, c * CH:(c + 1) * CH]
                        nc.vector.scalar_tensor_tensor(out=part, in0=relu[:, c % 2, :], scalar=0.0, in1=part,
                                                       op0=ALU.is_gt, op1=ALU.mult).then_inc(mask_done, 1)

                    def copy(g):
                        dve.wait_ge(odd_mm, (b * T + old) * (G // 2) + g // 2 + 1)
                        dve.wait_ge(av_mm, (b * T + old) * G + g - 1 + AV_CREDIT)
                        nc.vector.tensor_copy(attnT[:, 1, :], ps[:, 5, :]).then_inc(odd_out, 1)

                    if new is not None:
                        exponents(0)
                        exponents(1)
                        mask(0)
                    if old is not None:
                        copy(1)
                    if new is not None:
                        mask(1)
                        exponents(2)
                    if old is not None:
                        copy(3)
                    if new is not None:
                        mask(2)
                        exponents(3)
                    if old is not None:
                        copy(5)
                    if new is not None:
                        mask(3)
                    if old is not None:
                        copy(7)
                    if new is not None:
                        nc.vector.reduce_sum(zsum[:, h:h + 1], zpart[:, h, :], axis=AX.X)
                        dve.drain()
                        nc.vector.reciprocal(zinv[:, h:h + 1], zsum[:, h:h + 1])
                        dve.drain()
                        nc.vector.tensor_scalar(E[:, h, :], E[:, h, :], zinv[:, h:h + 1], 1e-8, ALU.mult,
                                                ALU.max).then_inc(clip_done, 1)

                step(0, None, 0)
                with dve.Fori(0, T // 2 - 1) as i:
                    step(i * 2 + 1, i * 2, 1)
                    step(i * 2 + 2, i * 2 + 1, 0)
                step(T - 1, T - 2, 1)
                step(None, T - 1, 0)
                for j in range(NB):
                    dve.wait_ge(lin_out, b * NB + j + 1)
                    nc.vector.scalar_tensor_tensor(out=lin[:, j % 2, :], in0=lin[:, j % 2, :], scalar=0.2,
                                                   in1=lin[:, j % 2, :], op0=ALU.mult, op1=ALU.max)
                    dve.drain()
                    part = x[:, ds(b * N + j * BANK, BANK)]
                    nc.vector.tensor_tensor(part, part, lin[:, j % 2, :], ALU.add).then_inc(residual_done, 1)
                dve.sem_inc(banks_free, 1)


S1 = 64
R1 = 8
L1_WEIGHTS = [("in_w", C), ("dt_w", R1), ("bc_w", 2 * S1), ("dtr_w", C), ("out_w", C), ("ident", C), ("ones", C),
              ("A", S1), ("conv_b", 1), ("gamma", 1), ("beta", 1), ("dt_b", 1), ("bc_b", 1), ("dtr_b", 1), ("D", 1)]
L1_AT, L1_WIDTH = columns(L1_WEIGHTS)
PARTS = 3
SEL = 32


def scan_layer(nc, x, weights, conv_weights, select):
    CH = 1024
    NC = N // CH
    CB = CH // BANK
    LAG = 3
    HALF = N // 2
    ctx = ExitStack()
    with ctx:
        sb = lambda name, shape, dt=F32: ctx.enter_context(nc.sbuf_tensor("l1_" + name, shape, dt))
        sem = lambda name: ctx.enter_context(nc.semaphore("l1_" + name))
        w = sb("w", [128, L1_WIDTH])
        wt = lambda name: w[:, L1_AT[name]]
        ident, ones = wt("ident"), wt("ones")
        sel = sb("sel", [PARTS * SEL, SEL * 128], BF16)
        taps = sb("taps", [128, 9, C])
        stack = sb("stack", [PARTS * SEL, 4, N], BF16)
        delta = sb("delta", [128, N])
        du = sb("du", [128, N])
        g = sb("g", [128, N])
        ring = sb("ring", [128, 10 * CH])
        slots = lambda at, n: ring[:, at * CH:(at + n) * CH].rearrange("p (s n) -> p s n", s=n)
        decay, h, hc, c_row = slots(0, 2), slots(2, 4), slots(6, 2), slots(8, 2)
        u = ring[:, 0:N]
        usq = ring[:, N:2 * N]
        bc = ring[:, N:N + HALF]
        parts = ring[:, N + HALF:N + HALF + PARTS * HALF // 2].bitcast(BF16).rearrange("p (a n) -> p a n", a=PARTS)
        dt_raw = du[0:R1, :]
        QT = N // 4
        soft = [du[:, i * QT:(i + 1) * QT] for i in range(3)]
        conv_raw = delta[:, 0:10 * C]
        carry = sb("carry", [128, S1])
        var = sb("var", [128, T])
        root = sb("root", [128, T])
        rstd = sb("rstd", [128, T])
        tmp = sb("tmp", [128, T])
        row_mean = sb("row_mean", [128, 1])
        ps = ctx.enter_context(nc.psum_tensor("l1_ps", [128, 8, BANK], F32))
        flat = lambda a, n: ps[:, a:a + n, :].rearrange("p a b -> p (a b)")
        b_row = [flat(0, CB), flat(2, CB)]
        c_psum = flat(4, CB)
        y_sum = flat(6, CB)

        weights_in = sem("weights_in"); setup = sem("setup"); A_ready = sem("A_ready")
        banks_free = sem("banks_free")
        u_mm = sem("u_mm"); u_out = sem("u_out"); squared = sem("squared"); var_mm = sem("var_mm")
        var_ready = sem("var_ready"); root_ready = sem("root_ready"); rstd_ready = sem("rstd_ready")
        rstd_mm = sem("rstd_mm"); u_scaled = sem("u_scaled"); u_ready = sem("u_ready")
        dt_mm = sem("dt_mm"); dt_out = sem("dt_out"); bc_mm = sem("bc_mm"); bc_out = sem("bc_out")
        bc_free = sem("bc_free"); parts_ready = sem("parts_ready"); stack_in = sem("stack_in")
        delta_mm = sem("delta_mm"); delta_out = sem("delta_out"); exp_ready = sem("exp_ready"); ln_ready = sem("ln_ready")
        soft_free = sem("soft_free")
        conv_mm = sem("conv_mm"); silu_out = sem("silu_out"); g_out = sem("g_out"); prep_done = sem("prep_done")
        b_mm = sem("b_mm"); c_mm = sem("c_mm"); c_ready = sem("c_ready"); decay_ready = sem("decay_ready")
        inp_done = sem("inp_done"); scan_done = sem("scan_done"); hc_done = sem("hc_done"); sum_mm = sem("sum_mm")
        y_out = sem("y_out"); out_mm = sem("out_mm")

        block = ctx.enter_context(nc.Block())

        @block.sync
        def _(sp):
            sp.dma_start(w[:], weights).then_inc(weights_in, 16)
            sp.dma_start(conv_raw, conv_weights).then_inc(weights_in, 16)
            sp.dma_start(sel[:], select).then_inc(weights_in, 16)
            with sp.Fori(0, B) as b:
                for hf in range(2):
                    sp.wait_ge(parts_ready, b * 2 + hf + 1)
                    for grp in range(4):
                        for a in range(PARTS):
                            sp.dma_start(stack[a * SEL:(a + 1) * SEL, grp, hf * HALF:(hf + 1) * HALF],
                                         parts[grp * SEL:(grp + 1) * SEL, a, :]).then_inc(stack_in, 16)

        @block.tensor
        def _(pe):
            pe.sem_inc(sum_mm, 2)
            pe.wait_ge(weights_in, 48)
            pe.wait_ge(setup, 1)
            with pe.Fori(0, B) as b:
                pe.wait_ge(banks_free, b + 1)
                for j in range(NB):
                    nc.tensor.matmul(ps[:, j, :], wt("in_w"), x[:, ds(b * N + j * BANK, BANK)], start=True,
                                     stop=True).then_inc(u_mm, 1)
                pe.wait_ge(squared, b + 1)
                for t in range(T):
                    ins = nc.tensor.matmul(ps[:, 0, t:t + 1], usq[:, t * 128:(t + 1) * 128], ones[:, 0:1], start=True,
                                           stop=True)
                ins.then_inc(var_mm, 1)
                pe.wait_ge(rstd_ready, b + 1)
                for t in range(T):
                    ins = nc.tensor.matmul(ps[:, t // 4, (t % 4) * 128:(t % 4 + 1) * 128],
                                           rstd[:, t:t + 1].broadcast_to([128, 128]), ident, start=True, stop=True)
                    if t % 4 == 3:
                        ins.then_inc(rstd_mm, 1)
                for j in range(NB):
                    pe.wait_ge(u_ready, b * NB + j + 1)
                    nc.tensor.matmul(ps[0:R1, j, :], wt("dt_w"), u[:, j * BANK:(j + 1) * BANK], start=True,
                                     stop=True).then_inc(dt_mm, 1)

                def bc_projection(j):
                    nc.tensor.matmul(ps[:, j, :], wt("bc_w"), u[:, j * BANK:(j + 1) * BANK], start=True,
                                     stop=True).then_inc(bc_mm, 1)

                for j in range(NB // 2):
                    pe.wait_ge(dt_out, b * NB + j + 1)
                    bc_projection(j)
                pe.wait_ge(dt_out, b * NB + NB)
                for j in range(NB):
                    if j < NB // 2:
                        pe.wait_ge(bc_out, b * NB + j + 1)
                    nc.tensor.matmul(ps[:, j, :], w[0:R1, L1_AT["dtr_w"]], dt_raw[:, j * BANK:(j + 1) * BANK],
                                     start=True, stop=True).then_inc(delta_mm, 1)
                for j in range(NB):
                    pe.wait_ge(delta_out, b * NB + j + 1)
                    xs = x[:, ds(b * N, N)].rearrange("p (r c) -> p r c", c=W)
                    out = ps[:, j, :].rearrange("p (r c) -> p r c", c=W)
                    order = [(0, 0)] + [(dy, dx) for dy in (-1, 0, 1) for dx in (-1, 0, 1) if (dy, dx) != (0, 0)]
                    for n, (dy, dx) in enumerate(order):
                        r0, r1 = max(8 * j, -dy), min(8 * j + 8, H - dy)
                        c0, c1 = max(0, -dx), min(W, W - dx)
                        ins = nc.tensor.matmul(out[:, r0 - 8 * j:r1 - 8 * j, c0:c1], taps[:, 3 * (dy + 1) + dx + 1, :],
                                               xs[:, r0 + dy:r1 + dy, c0 + dx:c1 + dx], start=n == 0, stop=n == 8)
                    ins.then_inc(conv_mm, 1)
                for j in range(NB // 2, NB):
                    pe.wait_ge(g_out, b * NB + j + 1)
                    bc_projection(j)

                unit = b * NC * S1
                def broadcasts(c, m, grp, i, s):
                    one_hot = sel[:, ds(i * 128, 128)]
                    pe.wait_ge(inp_done, unit + c * S1 + m + 1)
                    for k in range(CB):
                        ins = nc.tensor.matmul(b_row[s][:, k * BANK:(k + 1) * BANK], one_hot,
                                               stack[:, grp, c * CH + k * BANK:c * CH + (k + 1) * BANK], start=True,
                                               stop=True)
                    ins.then_inc(b_mm, 1)
                    pe.wait_ge(c_ready, unit + c * S1 + m + 1)
                    for k in range(CB):
                        ins = nc.tensor.matmul(c_psum[:, k * BANK:(k + 1) * BANK], one_hot,
                                               stack[:, 2 + grp, c * CH + k * BANK:c * CH + (k + 1) * BANK], start=True,
                                               stop=True)
                    ins.then_inc(c_mm, 1)

                def add_state(c, m, s, start=False, stop=False):
                    pe.wait_ge(hc_done, unit + c * S1 + m + 5)
                    for k in range(CB):
                        ins = nc.tensor.matmul(y_sum[:, k * BANK:(k + 1) * BANK], ident,
                                               hc[:, s, k * BANK:(k + 1) * BANK], start=start, stop=stop)
                    ins.then_inc(sum_mm, 1)

                pe.wait_ge(stack_in, b * (2 * 4 * PARTS * 16) + 2 * 4 * PARTS * 16 + 16)
                pe.wait_ge(bc_out, b * NB + NB)
                for c in range(NC):
                    for m in range(LAG + 1):
                        broadcasts(c, m, 0, m, m % 2)
                        if m < LAG:
                            if c:
                                add_state(c - 1, S1 - LAG + m, (S1 - LAG + m) % 2, stop=m == LAG - 1)
                        else:
                            pe.wait_ge(y_out, b * NC + c + 1)
                            add_state(c, 0, 0, start=True)
                    for grp in range(2):
                        with pe.Fori(0 if grp else LAG + 1, SEL - 1, 2) as i:
                            for s in range(2):
                                broadcasts(c, grp * SEL + i + s, grp, i + s, s)
                                add_state(c, grp * SEL + i + s - LAG, (s - LAG) % 2)
                for m in range(LAG):
                    add_state(NC - 1, S1 - LAG + m, (S1 - LAG + m) % 2, stop=m == LAG - 1)
                for j in range(NB):
                    if j % CB == 0:
                        pe.wait_ge(y_out, b * NC + j // CB + 2)
                    if j == 0:
                        pe.wait_ge(y_out, b * NC + NC + 1)
                    nc.tensor.matmul(ps[:, j, :], wt("out_w"), g[:, j * BANK:(j + 1) * BANK], start=True,
                                     stop=True).then_inc(out_mm, 1)

        @block.scalar
        def _(act):
            act.sem_inc(c_ready, 1)
            act.wait_ge(weights_in, 48)
            nc.scalar.activation(wt("A"), wt("A"), ACT.Exp).then_inc(A_ready, 1)
            act.wait_ge(setup, 1)
            with act.Fori(0, B) as b:
                for j in range(NB):
                    act.wait_ge(u_mm, b * NB + j + 1)
                    nc.scalar.activation(u[:, j * BANK:(j + 1) * BANK], ps[:, j, :], ACT.Identity).then_inc(u_out, 1)
                act.wait_ge(var_ready, b + 1)
                nc.scalar.activation(root[:], var[:], ACT.Sqrt).then_inc(root_ready, 1)
                for j in range(NB):
                    act.wait_ge(u_scaled, b * NB + j + 1)
                    part = u[:, j * BANK:(j + 1) * BANK]
                    nc.scalar.activation(part, part, ACT.Identity, bias=wt("beta")).then_inc(u_ready, 1)
                for j in range(NB):
                    act.wait_ge(dt_mm, b * NB + j + 1)
                    nc.scalar.activation(dt_raw[:, j * BANK:(j + 1) * BANK], ps[0:R1, j, :], ACT.Identity,
                                         bias=w[0:R1, L1_AT["dt_b"]]).then_inc(dt_out, 1)

                def bc_copy(j):
                    act.wait_ge(bc_mm, b * NB + j + 1)
                    act.wait_ge(bc_free, b * 2 + j // (NB // 2) + 1)
                    nc.scalar.activation(bc[:, j % (NB // 2) * BANK:(j % (NB // 2) + 1) * BANK], ps[:, j, :],
                                         ACT.Identity, bias=wt("bc_b")).then_inc(bc_out, 1)

                for j in range(NB // 2):
                    bc_copy(j)
                for j in range(NB):
                    act.wait_ge(delta_mm, b * NB + j + 1)
                    nc.scalar.activation(delta[:, j * BANK:(j + 1) * BANK], ps[:, j, :], ACT.Identity,
                                         bias=wt("dtr_b")).then_inc(delta_out, 1)
                act.drain()
                for i in range(4):
                    act.wait_ge(soft_free, b * 4 + i + 1)
                    nc.scalar.activation(soft[0], delta[:, i * QT:(i + 1) * QT], ACT.Abs)
                    act.drain()
                    nc.scalar.activation(soft[0], soft[0], ACT.Exp, scale=-1.0).then_inc(exp_ready, 1)
                    act.drain()
                    nc.scalar.activation(soft[1], soft[0], ACT.Ln, bias=1.0).then_inc(ln_ready, 1)
                for j in range(NB):
                    act.wait_ge(conv_mm, b * NB + j + 1)
                    nc.scalar.activation(g[:, j * BANK:(j + 1) * BANK], ps[:, j, :], ACT.Silu,
                                         bias=wt("conv_b")).then_inc(silu_out, 1)
                for j in range(NB // 2, NB):
                    bc_copy(j)
                act.wait_ge(prep_done, b + 1)
                for c in range(NC):
                    with act.Fori(0, S1 - 1, 2) as n:
                        for s in range(2):
                            count = (b * NC + c) * S1 + n + s
                            act.wait_ge(scan_done, count + 1)
                            nc.scalar.activation(decay[:, s, :], delta[:, c * CH:(c + 1) * CH], ACT.Exp,
                                                 scale=wt("A")[:, ds(n + s, 1)]).then_inc(decay_ready, 1)
                            act.wait_ge(c_mm, count + 1)
                            act.wait_ge(hc_done, count + 3)
                            nc.scalar.activation(c_row[:, s, :], c_psum, ACT.Copy).then_inc(c_ready, 1)

        @block.gpsimd
        def _(pool):
            pool.sem_inc(hc_done, 4)
            with pool.Fori(0, B * NC * S1 - 3, 4) as n:
                for s in range(4):
                    pool.wait_ge(c_ready, n + s + 2)
                    pool.wait_ge(scan_done, n + s + 3)
                    pool.wait_ge(sum_mm, n + s + 1)
                    nc.gpsimd.tensor_tensor(hc[:, s % 2, :], h[:, s, :], c_row[:, s % 2, :], ALU.mult).then_inc(hc_done, 1)

        @block.vector
        def _(dve):
            dve.sem_inc(banks_free, 1)
            dve.sem_inc(bc_free, 1)
            dve.sem_inc(soft_free, 1)
            dve.sem_inc(inp_done, 2)
            dve.sem_inc(scan_done, 2)
            dve.sem_inc(y_out, 1)
            dve.sem_inc(stack_in, 16)
            dve.wait_ge(weights_in, 48)
            nc.vector.reduce_sum(row_mean[:], wt("in_w"), axis=AX.X)
            dve.drain()
            nc.vector.tensor_scalar(row_mean[:], row_mean[:], 1.0 / C, None, ALU.mult)
            dve.drain()
            nc.vector.tensor_scalar(wt("in_w"), wt("in_w"), row_mean[:], None, ALU.subtract)
            nc.vector.tensor_tensor(taps[:], conv_raw[:, C:].rearrange("p (t c) -> p t c", c=C),
                                    conv_raw[:, 0:C].unsqueeze(1).broadcast_to([128, 9, C]), ALU.mult)
            dve.wait_ge(A_ready, 1)
            nc.vector.tensor_scalar(wt("A"), wt("A"), -1.0, None, ALU.mult).then_inc(setup, 1)
            with dve.Fori(0, B) as b:
                dve.wait_ge(u_out, b * NB + NB)
                nc.vector.tensor_tensor(usq, u, u, ALU.mult).then_inc(squared, 1)
                dve.wait_ge(var_mm, b + 1)
                nc.vector.tensor_scalar(var[:], ps[:, 0, 0:T], 1.0 / C, 1e-5, ALU.mult, ALU.add).then_inc(var_ready, 1)
                dve.wait_ge(root_ready, b + 1)
                nc.vector.reciprocal(rstd[:], root[:])
                dve.drain()
                nc.vector.tensor_tensor(tmp[:], var[:], rstd[:], ALU.mult)
                dve.drain()
                nc.vector.tensor_tensor(tmp[:], tmp[:], rstd[:], ALU.mult)
                dve.drain()
                nc.vector.tensor_scalar(tmp[:], tmp[:], -0.5, 1.5, ALU.mult, ALU.add)
                dve.drain()
                nc.vector.tensor_tensor(rstd[:], rstd[:], tmp[:], ALU.mult).then_inc(rstd_ready, 1)
                for j in range(NB):
                    dve.wait_ge(rstd_mm, b * NB + j + 1)
                    part = u[:, j * BANK:(j + 1) * BANK]
                    nc.vector.scalar_tensor_tensor(out=part, in0=part, scalar=wt("gamma"), in1=ps[:, j, :],
                                                   op0=ALU.mult, op1=ALU.mult).then_inc(u_scaled, 1)

                def split(hf):
                    dve.wait_ge(bc_out, b * NB + (hf + 1) * (NB // 2))
                    dve.wait_ge(stack_in, (b * 2 + hf) * (4 * PARTS * 16) + 16)
                    for a in range(PARTS):
                        ins = nc.vector.tensor_copy(parts[:, a, :], bc)
                        dve.drain()
                        if a < PARTS - 1:
                            nc.vector.tensor_tensor(bc, bc, parts[:, a, :], ALU.subtract)
                            dve.drain()
                    dve.sem_inc(parts_ready, 1)
                    dve.sem_inc(bc_free, 1)

                split(0)
                for i in range(4):
                    part = delta[:, i * QT:(i + 1) * QT]
                    dve.wait_ge(exp_ready, b * 4 + i + 1)
                    nc.vector.tensor_scalar(soft[2], soft[0], 1.0, 1.0, ALU.add, ALU.subtract)
                    dve.drain()
                    nc.vector.tensor_tensor(soft[2], soft[0], soft[2], ALU.subtract)
                    dve.wait_ge(ln_ready, b * 4 + i + 1)
                    nc.vector.scalar_tensor_tensor(out=part, in0=part, scalar=0.0, in1=soft[1], op0=ALU.max, op1=ALU.add)
                    dve.drain()
                    nc.vector.tensor_tensor(part, part, soft[2], ALU.add).then_inc(soft_free, 1)
                dve.drain()
                nc.vector.tensor_tensor(du[:], delta[:], u, ALU.mult)
                for j in range(NB):
                    part = g[:, j * BANK:(j + 1) * BANK]
                    dve.wait_ge(silu_out, b * NB + j + 1)
                    nc.vector.scalar_tensor_tensor(out=part, in0=ps[:, j, :], scalar=wt("conv_b"), in1=part,
                                                   op0=ALU.add, op1=ALU.mult).then_inc(g_out, 1)
                dve.drain()
                nc.vector.scalar_tensor_tensor(out=g[:], in0=u, scalar=wt("D"), in1=g[:], op0=ALU.mult, op1=ALU.add)
                split(1)
                nc.vector.memset(carry[:], 0.0)
                dve.drain()
                dve.wait_ge(bc_mm, b * NB + NB)
                dve.sem_inc(prep_done, 1)
                unit = b * NC * S1

                def state_input(c, m, s):
                    dve.wait_ge(b_mm, unit + c * S1 + m + 1)
                    dve.wait_ge(hc_done, unit + c * S1 + m + 1)
                    dve.wait_ge(inp_done, unit + c * S1 + m + 2)
                    nc.vector.tensor_tensor(h[:, s, :], du[:, c * CH:(c + 1) * CH], b_row[s % 2], ALU.mult)\
                        .then_inc(inp_done, 1)

                def scan(c, m, s):
                    dve.wait_ge(inp_done, unit + c * S1 + m + 3)
                    dve.wait_ge(decay_ready, unit + c * S1 + m + 1)
                    nc.vector.tensor_tensor_scan(h[:, s, :], decay[:, s % 2, :], h[:, s, :], carry[:, ds(m, 1)],
                                                 ALU.mult, ALU.add).then_inc(scan_done, 1)

                def keep(c, m, s):
                    dve.wait_ge(scan_done, unit + c * S1 + m + 3)
                    nc.vector.tensor_scalar(carry[:, ds(m, 1)], h[:, s, CH - 1:CH], 1.0, None, ALU.mult)

                def add_y(c):
                    dve.wait_ge(sum_mm, unit + c * S1 + S1 + 2)
                    part = g[:, c * CH:(c + 1) * CH]
                    nc.vector.tensor_tensor(part, part, y_sum, ALU.add).then_inc(y_out, 1)

                for c in range(NC):
                    for m in range(4):
                        state_input(c, m, m)
                        for lag, run in ((1, scan), (2, keep)):
                            if m >= lag:
                                run(c, m - lag, m - lag)
                            elif c:
                                run(c - 1, S1 + m - lag, 4 + m - lag)
                    if c:
                        add_y(c - 1)
                    with dve.Fori(4, S1 - 3, 4) as m:
                        for s in range(4):
                            state_input(c, m + s, s)
                            scan(c, m + s - 1, (s - 1) % 4)
                            keep(c, m + s - 2, (s - 2) % 4)
                scan(NC - 1, S1 - 1, 3)
                add_y(NC - 1)
                for j in range(NB):
                    dve.wait_ge(out_mm, b * NB + j + 1)
                    part = x[:, ds(b * N + j * BANK, BANK)]
                    nc.vector.tensor_tensor(part, part, ps[:, j, :], ALU.add)
                dve.drain()
                dve.sem_inc(banks_free, 1)


L2_WEIGHTS = [("h_w", C), ("f_w", 1), ("g_w", 1), ("h_b", C), ("f_b", 1), ("g_b", 1)]
L2_AT, L2_WIDTH = columns(L2_WEIGHTS)


def rank_one_attention_layer(nc, x, weights):
    ctx = ExitStack()
    with ctx:
        sb = lambda name, shape, dt=F32: ctx.enter_context(nc.sbuf_tensor("l2_" + name, shape, dt))
        sem = lambda name: ctx.enter_context(nc.semaphore("l2_" + name))
        w = sb("w", [128, L2_WIDTH])
        wt = lambda name: w[:, L2_AT[name]]
        xb = sb("xb", [128, N])
        g = sb("g", [128, N])
        hT = sb("hT", [128, N])
        E = sb("E", [128, 2, N])
        hs = sb("hs", [128, 2, C])
        f = sb("f", [128, T])
        neg_max = sb("neg_max", [128, T])
        tmp = sb("tmp", [128, T])
        g_max = sb("g_max", [128, 1])
        g_min = sb("g_min", [128, 1])
        zsum = sb("zsum", [128, 2])
        zinv = sb("zinv", [128, 2])
        ps = ctx.enter_context(nc.psum_tensor("l2_ps", [128, 8, BANK], F32))

        weights_in = sem("weights_in"); xb_ready = sem("xb_ready"); bank_free = sem("bank_free")
        g_mm = sem("g_mm"); g_out = sem("g_out"); f_mm = sem("f_mm"); f_out = sem("f_out")
        h_mm = sem("h_mm"); h_out = sem("h_out"); max_ready = sem("max_ready")
        exp_ready = sem("exp_ready"); hs_ready = sem("hs_ready"); tile_mm = sem("tile_mm"); sum_mm = sem("sum_mm")

        block = ctx.enter_context(nc.Block())

        @block.sync
        def _(sp):
            sp.dma_start(w[:], weights).then_inc(weights_in, 16)

        @block.tensor
        def _(pe):
            pe.sem_inc(tile_mm, 2)
            pe.wait_ge(weights_in, 16)
            with pe.Fori(0, B) as b:
                for j in range(NB):
                    pe.wait_ge(bank_free, b * NB + j + 1)
                    nc.tensor.matmul(ps[:, j, :], wt("g_w").broadcast_to([128, 128]),
                                     x[:, ds(b * N + j * BANK, BANK)], start=True, stop=True).then_inc(g_mm, 1)
                pe.wait_ge(xb_ready, b + 1)
                pe.wait_ge(g_out, b * NB + 1)
                for t in range(T):
                    ins = nc.tensor.matmul(ps[:, 0, t:t + 1], xb[:, t * 128:(t + 1) * 128], wt("f_w"), start=True,
                                           stop=True)
                ins.then_inc(f_mm, 1)
                for n in range(NB):
                    j = (n + 1) % NB
                    if j:
                        pe.wait_ge(g_out, b * NB + j + 1)
                    else:
                        pe.wait_ge(f_out, b + 1)
                    for a in range(4):
                        t = 4 * j + a
                        ins = nc.tensor.matmul(ps[:, j, a * 128:(a + 1) * 128], xb[:, t * 128:(t + 1) * 128],
                                               wt("h_w"), start=True, stop=True)
                    ins.then_inc(h_mm, 1)
                pe.wait_ge(h_out, b * NB + NB)

                def tile(t, s, start=False, stop=False):
                    pe.wait_ge(hs_ready, b * T + t + 1)
                    for j in range(NB):
                        ins = nc.tensor.matmul(ps[:, j, :], hs[:, s, :], E[:, s, j * BANK:(j + 1) * BANK], start=start,
                                               stop=stop)
                        if stop:
                            ins.then_inc(sum_mm, 1)
                    if not stop:
                        ins.then_inc(tile_mm, 1)

                tile(0, 0, start=True)
                with pe.Fori(1, T - 2, 2) as t:
                    tile(t, 1)
                    tile(t + 1, 0)
                tile(T - 1, 1, stop=True)
                pe.wait_ge(sum_mm, b * NB + NB)
                pe.sem_inc(tile_mm, 1)

        @block.scalar
        def _(act):
            act.wait_ge(weights_in, 16)
            with act.Fori(0, B) as b:
                for j in range(NB):
                    act.wait_ge(g_mm, b * NB + j + 1)
                    nc.scalar.activation(g[:, j * BANK:(j + 1) * BANK], ps[:, j, :], ACT.Identity,
                                         bias=wt("g_b")).then_inc(g_out, 1)
                act.wait_ge(max_ready, b + 1)
                with act.Fori(0, T - 1, 2) as t:
                    for s in range(2):
                        act.wait_ge(tile_mm, b * T + t + s + 1)
                        nc.scalar.activation(E[:, s, :], g[:], ACT.Exp, scale=f[:, ds(t + s, 1)],
                                             bias=neg_max[:, ds(t + s, 1)],
                                             accum_out=zsum[:, s:s + 1]).then_inc(exp_ready, 1)

        @block.vector
        def _(dve):
            dve.sem_inc(bank_free, NB)
            dve.wait_ge(weights_in, 16)
            with dve.Fori(0, B) as b:
                nc.vector.tensor_copy(xb[:], x[:, ds(b * N, N)]).then_inc(xb_ready, 1)
                dve.wait_ge(f_mm, b + 1)
                nc.vector.tensor_scalar(f[:], ps[:, 0, 0:T], wt("f_b"), None, ALU.add).then_inc(f_out, 1)
                for n in range(NB):
                    j = (n + 1) % NB
                    dve.wait_ge(h_mm, b * NB + n + 1)
                    nc.vector.tensor_tensor(hT[:, j * BANK:(j + 1) * BANK].rearrange("p (a c) -> p a c", a=4),
                                            ps[:, j, :].rearrange("p (a c) -> p a c", a=4),
                                            wt("h_b").unsqueeze(1).broadcast_to([128, 4, C]), ALU.add).then_inc(h_out, 1)
                dve.wait_ge(g_out, b * NB + NB)
                nc.vector.reduce_max(g_max[:], g[:], axis=AX.X)
                nc.vector.tensor_reduce(g_min[:], g[:], AX.X, ALU.min)
                dve.drain()
                nc.vector.tensor_scalar(neg_max[:], f[:], g_max[:], None, ALU.mult)
                nc.vector.tensor_scalar(tmp[:], f[:], g_min[:], None, ALU.mult)
                dve.drain()
                nc.vector.tensor_tensor(neg_max[:], neg_max[:], tmp[:], ALU.max)
                dve.drain()
                nc.vector.tensor_scalar(neg_max[:], neg_max[:], -1.0, None, ALU.mult).then_inc(max_ready, 1)
                with dve.Fori(0, T - 1, 2) as t:
                    for s in range(2):
                        dve.wait_ge(exp_ready, b * T + t + s + 1)
                        nc.vector.reciprocal(zinv[:, s:s + 1], zsum[:, s:s + 1])
                        dve.drain()
                        nc.vector.tensor_scalar(hs[:, s, :], hT[:, ds((t + s) * C, C)], zinv[:, s:s + 1], None,
                                                ALU.mult).then_inc(hs_ready, 1)
                for j in range(NB):
                    dve.wait_ge(sum_mm, b * NB + j + 1)
                    part = x[:, ds(b * N + j * BANK, BANK)]
                    nc.vector.tensor_tensor(part, part, ps[:, j, :], ALU.add).then_inc(bank_free, 1)
                dve.drain()


DI = 256
TI = DI // 128
S3 = 16
R3 = 8
K3 = 4
PAD = K3 - 1
GROUP = 32
L3_WEIGHTS = [("u_w", DI), ("z_w", DI), ("bc_w", TI * PARTS * SEL), ("dt_w", TI * R3), ("dtr_w", DI), ("out_w", DI),
              ("ident", C), ("A", TI * S3), ("conv_b", TI), ("dtr_b", TI), ("D", TI), ("gn_w", 1), ("gn_b", 1),
              ("group_mean", C), ("below_top", 2)]
L3_AT, L3_WIDTH = columns(L3_WEIGHTS)


def two_way_scan_layer(nc, xp, weights, conv_weights, select, out):
    L = B * N
    CH = 1024
    NCH = L // CH
    CB = CH // BANK
    UNITS = S3 * TI
    ctx = ExitStack()
    with ctx:
        sb = lambda name, shape, dt=F32: ctx.enter_context(nc.sbuf_tensor("l3_" + name, shape, dt))
        sem = lambda name: ctx.enter_context(nc.semaphore("l3_" + name))
        recon_dram = nc.dram_tensor("l3_recon_dram", [128, L], F32, kind="Internal").ap()
        w = sb("w", [128, L3_WIDTH])
        wt = lambda name: w[:, L3_AT[name]]
        ident = wt("ident")
        col = lambda name, i, n=1: w[:, L3_AT[name].start + i:L3_AT[name].start + i + n]
        sel = sb("sel", [PARTS * SEL, SEL * 128], BF16)
        taps = sb("taps", [128, K3, DI])
        ring = sb("ring", [128, 10 * CH])
        slots = lambda at, n: ring[:, at * CH:(at + n) * CH].rearrange("p (s n) -> p s n", s=n)
        decay, h, hc, c_row = slots(0, 2), slots(2, 4), slots(6, 2), slots(8, 2)
        conv_rows = ring[:, 0:K3 * DI]
        u = sb("u", [128, TI, CH])
        gate = sb("gate", [128, TI, CH])
        delta = sb("delta", [128, TI, CH])
        du = sb("du", [128, TI, CH])
        z1 = slots(2, 2)
        z2 = slots(4, 2)
        z3 = slots(6, 2)
        dt_raw = sb("dt_raw", [R3, CH])
        rest = sb("rest", [PARTS * SEL, CH])
        part = sb("part", [PARTS * SEL, CH], BF16)
        stack = sb("stack", [PARTS * SEL, CH], BF16)
        recon = sb("recon", [128, CH])
        loaded = sb("loaded", [128, CH])
        carry = sb("carry", [128, UNITS])
        stats = sb("stats", [128, L // BANK, 6])
        ps = ctx.enter_context(nc.psum_tensor("l3_ps", [128, 8, BANK], F32))
        flat = lambda a, n: ps[:, a:a + n, :].rearrange("p a b -> p (a b)")
        b_psum, c_psum = flat(0, CB), flat(2, CB)
        y_sum = [flat(4, CB), flat(6, CB)]

        weights_in = sem("weights_in"); setup = sem("setup"); A_ready = sem("A_ready")
        chunk_done = sem("chunk_done")
        u_mm = sem("u_mm"); u_out = sem("u_out"); z_mm = sem("z_mm"); gate_out = sem("gate_out")
        bc_mm = sem("bc_mm"); dt_mm = sem("dt_mm"); dt_out = sem("dt_out"); high = sem("high"); rest_ready = sem("rest_ready")
        middle = sem("middle"); stack_ready = sem("stack_ready")
        delta_mm = sem("delta_mm"); delta_out = sem("delta_out"); exp_ready = sem("exp_ready"); ln_ready = sem("ln_ready")
        prep_done = sem("prep_done")
        b_mm = sem("b_mm"); c_mm = sem("c_mm"); c_ready = sem("c_ready"); decay_ready = sem("decay_ready")
        inp_done = sem("inp_done"); scan_done = sem("scan_done"); hc_done = sem("hc_done"); sum_mm = sem("sum_mm")
        gated = sem("gated"); out_mm = sem("out_mm"); recon_ready = sem("recon_ready")
        recon_stored = sem("recon_stored"); recon_loaded = sem("recon_loaded")

        with nc.Block() as block:

            @block.sync
            def _(sp):
                sp.dma_start(w[:], weights).then_inc(weights_in, 16)
                sp.dma_start(conv_rows, conv_weights).then_inc(weights_in, 16)
                sp.dma_start(sel[:], select).then_inc(weights_in, 16)
                with sp.Fori(0, NCH) as c:
                    sp.wait_ge(recon_ready, c + 1)
                    sp.dma_start(recon_dram[:, ds(c * CH, CH)], recon[:]).then_inc(recon_stored, 16)
                sp.wait_ge(recon_stored, 16 * NCH + 16)
                with sp.Fori(0, NCH) as c:
                    sp.wait_ge(chunk_done, c + (NCH + 1))
                    sp.dma_start(loaded[:], recon_dram[:, ds((c - (NCH - 1)) * -CH, CH)]).then_inc(recon_loaded, 16)
                    sp.wait_ge(recon_ready, c + (NCH + 1))
                    sp.dma_start(recon_dram[:, ds((c - (NCH - 1)) * -CH, CH)], recon[:]).then_inc(recon_stored, 16)
                sp.wait_ge(recon_stored, 2 * 16 * NCH + 16)

            @block.tensor
            def _(pe):
                pe.sem_inc(sum_mm, 2)
                pe.wait_ge(weights_in, 48)
                pe.wait_ge(setup, 1)
                for d in range(2):
                    with pe.Fori(0, NCH) as c:
                        K = c + d * NCH
                        at = L - CH - c * CH if d else c * CH
                        pe.wait_ge(chunk_done, K + 1)
                        for e in range(TI):
                            for j in range(CB):
                                for k in range(K3):
                                    shift = PAD - k if d else k - PAD
                                    ins = nc.tensor.matmul(ps[:, e * CB + j, :], taps[:, k, e * 128:(e + 1) * 128],
                                                           xp[:, ds(at + (PAD + shift + j * BANK), BANK)], start=k == 0,
                                                           stop=k == K3 - 1)
                                ins.then_inc(u_mm, 1)
                        for e in range(TI):
                            for j in range(CB):
                                nc.tensor.matmul(ps[:, 4 + e * CB + j, :], col("z_w", e * 128, 128),
                                                 xp[:, ds(at + (PAD + j * BANK), BANK)], start=True,
                                                 stop=True).then_inc(z_mm, 1)
                        pe.wait_ge(u_out, K * 4 + 4)
                        for j in range(CB):
                            for e in range(TI):
                                ins = nc.tensor.matmul(ps[0:PARTS * SEL, j, :], col("bc_w", e * PARTS * SEL, PARTS * SEL),
                                                       u[:, e, j * BANK:(j + 1) * BANK], start=e == 0, stop=e == TI - 1)
                        ins.then_inc(bc_mm, 1)
                        for j in range(CB):
                            for e in range(TI):
                                ins = nc.tensor.matmul(ps[0:R3, 2 + j, :], col("dt_w", e * R3, R3),
                                                       u[:, e, j * BANK:(j + 1) * BANK], start=e == 0, stop=e == TI - 1)
                        ins.then_inc(dt_mm, 1)
                        pe.wait_ge(dt_out, K + 1)
                        pe.wait_ge(gate_out, K * 4 + 4)
                        for e in range(TI):
                            for j in range(CB):
                                nc.tensor.matmul(ps[:, 4 + e * CB + j, :],
                                                 w[0:R3, L3_AT["dtr_w"].start + e * 128:L3_AT["dtr_w"].start + (e + 1) * 128],
                                                 dt_raw[:, j * BANK:(j + 1) * BANK], start=True,
                                                 stop=True).then_inc(delta_mm, 1)

                        def broadcasts(n):
                            pe.wait_ge(inp_done, (K * S3 + n) * TI + 2)
                            for j in range(CB):
                                ins = nc.tensor.matmul(b_psum[:, j * BANK:(j + 1) * BANK], sel[:, ds(n * 128, 128)],
                                                       stack[:, j * BANK:(j + 1) * BANK], start=True, stop=True)
                            ins.then_inc(b_mm, 1)
                            pe.wait_ge(c_ready, K * S3 + n + 1)
                            for j in range(CB):
                                ins = nc.tensor.matmul(c_psum[:, j * BANK:(j + 1) * BANK],
                                                       sel[:, ds(n * 128 + S3 * 128, 128)],
                                                       stack[:, j * BANK:(j + 1) * BANK], start=True, stop=True)
                            ins.then_inc(c_mm, 1)

                        def add_state(n, start=False, stop=False):
                            for e in range(TI):
                                pe.wait_ge(hc_done, (K * S3 + n) * TI + e + 5)
                                for j in range(CB):
                                    ins = nc.tensor.matmul(y_sum[e][:, j * BANK:(j + 1) * BANK], ident,
                                                           hc[:, e, j * BANK:(j + 1) * BANK], start=start, stop=stop)
                                ins.then_inc(sum_mm, 1)

                        pe.wait_ge(stack_ready, K + 1)
                        pe.wait_ge(delta_out, K * 4 + 4)
                        broadcasts(0)
                        broadcasts(1)
                        broadcasts(2)
                        add_state(0, start=True)
                        with pe.Fori(3, S3) as n:
                            broadcasts(n)
                            add_state(n - 2)
                        add_state(S3 - 2)
                        add_state(S3 - 1, stop=True)
                        pe.wait_ge(gated, K + 1)
                        for j in range(CB):
                            for e in range(TI):
                                ins = nc.tensor.matmul(ps[:, j, :], col("out_w", e * 128, 128),
                                                       gate[:, e, j * BANK:(j + 1) * BANK], start=e == 0,
                                                       stop=e == TI - 1)
                        ins.then_inc(out_mm, 1)

            @block.scalar
            def _(act):
                act.sem_inc(c_ready, 1)
                act.wait_ge(weights_in, 48)
                nc.scalar.activation(wt("A"), wt("A"), ACT.Exp).then_inc(A_ready, 1)
                act.wait_ge(setup, 1)
                with act.Fori(0, 2 * NCH) as K:
                    for e in range(TI):
                        for j in range(CB):
                            act.wait_ge(u_mm, K * 4 + (e * CB + j + 1))
                            nc.scalar.activation(u[:, e, j * BANK:(j + 1) * BANK], ps[:, e * CB + j, :], ACT.Silu,
                                                 bias=col("conv_b", e)).then_inc(u_out, 1)
                    for e in range(TI):
                        for j in range(CB):
                            act.wait_ge(z_mm, K * 4 + (e * CB + j + 1))
                            nc.scalar.activation(gate[:, e, j * BANK:(j + 1) * BANK], ps[:, 4 + e * CB + j, :],
                                                 ACT.Silu).then_inc(gate_out, 1)
                    act.wait_ge(bc_mm, K + 1)
                    nc.scalar.activation(part[:], flat(0, CB)[0:PARTS * SEL, :], ACT.Copy).then_inc(high, 1)
                    act.wait_ge(dt_mm, K + 1)
                    nc.scalar.activation(dt_raw[:], flat(2, CB)[0:R3, :], ACT.Copy).then_inc(dt_out, 1)
                    act.wait_ge(rest_ready, K + 1)
                    nc.scalar.activation(part[:], rest[:], ACT.Copy).then_inc(middle, 1)
                    for e in range(TI):
                        for j in range(CB):
                            act.wait_ge(delta_mm, K * 4 + (e * CB + j + 1))
                            nc.scalar.activation(delta[:, e, j * BANK:(j + 1) * BANK], ps[:, 4 + e * CB + j, :],
                                                 ACT.Identity, bias=col("dtr_b", e)).then_inc(delta_out, 1)
                    act.drain()
                    nc.scalar.activation(z1, delta[:], ACT.Abs)
                    act.drain()
                    nc.scalar.activation(z1, z1, ACT.Exp, scale=-1.0).then_inc(exp_ready, 1)
                    act.drain()
                    nc.scalar.activation(z2, z1, ACT.Ln, bias=1.0).then_inc(ln_ready, 1)
                    act.wait_ge(prep_done, K + 1)
                    with act.Fori(0, S3 - 1, 2) as n:
                        for s in range(2):
                            for e in range(TI):
                                act.wait_ge(scan_done, (K * S3 + n) * TI + (s * TI + e + 1))
                                nc.scalar.activation(decay[:, e, :], delta[:, e, :], ACT.Exp,
                                                     scale=wt("A")[:, ds(n + (e * S3 + s), 1)]).then_inc(decay_ready, 1)
                                if e == 0:
                                    act.wait_ge(c_mm, K * S3 + n + (s + 1))
                                    act.wait_ge(hc_done, (K * S3 + n) * TI + (s * TI + 2))
                                    nc.scalar.activation(c_row[:, s, :], c_psum, ACT.Copy).then_inc(c_ready, 1)

            @block.gpsimd
            def _(pool):
                pool.sem_inc(hc_done, 4)
                with pool.Fori(0, 2 * NCH * S3 - 1, 2) as n:
                    for s in range(4):
                        if s % TI == 0:
                            pool.wait_ge(c_ready, n + (s // 2 + 2))
                        pool.wait_ge(scan_done, n * TI + (s + 3))
                        pool.wait_ge(sum_mm, n * TI + (s + 1))
                        nc.gpsimd.tensor_tensor(hc[:, s % 2, :], h[:, s, :], c_row[:, s // 2, :], ALU.mult)\
                            .then_inc(hc_done, 1)

            @block.vector
            def _(dve):
                dve.sem_inc(chunk_done, 1)
                dve.sem_inc(inp_done, 2)
                dve.sem_inc(scan_done, 2)
                dve.sem_inc(recon_stored, 16)
                dve.wait_ge(weights_in, 48)
                for k in range(K3):
                    nc.vector.tensor_tensor(taps[:, k, :], conv_rows[:, k * DI:(k + 1) * DI], wt("u_w"), ALU.mult)
                dve.wait_ge(A_ready, 1)
                nc.vector.tensor_scalar(wt("A"), wt("A"), -1.0, None, ALU.mult).then_inc(setup, 1)
                for d in range(2):
                    nc.vector.memset(carry[:], 0.0)
                    dve.drain()
                    with dve.Fori(0, NCH) as c:
                        K = c + d * NCH
                        dve.wait_ge(high, K + 1)
                        nc.vector.scalar_tensor_tensor(out=rest[:], in0=part[:], scalar=col("below_top", 0)[0:PARTS * SEL, :],
                                                       in1=flat(0, CB)[0:PARTS * SEL, :], op0=ALU.mult,
                                                       op1=ALU.add).then_inc(rest_ready, 1)
                        dve.wait_ge(middle, K + 1)
                        nc.vector.scalar_tensor_tensor(out=stack[:], in0=part[:], scalar=col("below_top", 1)[0:PARTS * SEL, :],
                                                       in1=rest[:], op0=ALU.mult, op1=ALU.add).then_inc(stack_ready, 1)
                        dve.wait_ge(exp_ready, K + 1)
                        nc.vector.tensor_scalar(z3, z1, 1.0, 1.0, ALU.add, ALU.subtract)
                        dve.drain()
                        nc.vector.tensor_tensor(z3, z1, z3, ALU.subtract)
                        dve.wait_ge(ln_ready, K + 1)
                        nc.vector.scalar_tensor_tensor(out=delta[:], in0=delta[:], scalar=0.0, in1=z2, op0=ALU.max,
                                                       op1=ALU.add)
                        dve.drain()
                        nc.vector.tensor_tensor(delta[:], delta[:], z3, ALU.add)
                        dve.drain()
                        nc.vector.tensor_tensor(du[:], delta[:], u[:], ALU.mult).then_inc(prep_done, 1)
                        dve.drain()
                        order = slice(None, None, -1) if d else slice(None)
                        last = 0 if d else CH - 1

                        def state_input(n, e, s):
                            if e == 0:
                                dve.wait_ge(b_mm, K * S3 + n + 1)
                            unit = (K * S3 + n) * TI + e
                            dve.wait_ge(hc_done, unit + 1)
                            dve.wait_ge(inp_done, unit + 2)
                            nc.vector.tensor_tensor(h[:, s, :], du[:, e, :], b_psum, ALU.mult).then_inc(inp_done, 1)

                        def scan(n, e, s):
                            unit = (K * S3 + n) * TI + e
                            dve.wait_ge(inp_done, unit + 3)
                            dve.wait_ge(decay_ready, unit + 1)
                            nc.vector.tensor_tensor_scan(h[:, s, order], decay[:, e, order], h[:, s, order],
                                                         carry[:, ds(n + e * S3, 1)], ALU.mult,
                                                         ALU.add).then_inc(scan_done, 1)

                        def keep(n, e, s):
                            dve.wait_ge(scan_done, (K * S3 + n) * TI + e + 3)
                            nc.vector.tensor_scalar(carry[:, ds(n + e * S3, 1)], h[:, s, last:last + 1], 1.0, None,
                                                    ALU.mult)

                        state_input(0, 0, 0)
                        state_input(0, 1, 1)
                        scan(0, 0, 0)
                        for s in (2, 3):
                            state_input(1, s % 2, s)
                            scan((s - 1) // 2, (s - 1) % 2, s - 1)
                            keep((s - 2) // 2, s % 2, s - 2)
                        with dve.Fori(2, S3 - 1, 2) as n:
                            for s in range(4):
                                state_input(n + s // 2, s % 2, s)
                                scan(n + (s - 1) // 2, (s - 1) % 2, (s - 1) % 4)
                                keep(n + (s - 2) // 2, s % 2, (s - 2) % 4)
                        scan(S3 - 1, 1, 3)
                        keep(S3 - 1, 0, 2)
                        keep(S3 - 1, 1, 3)
                        for e in range(TI):
                            dve.wait_ge(sum_mm, (K * S3 + S3) * TI + 2)
                            nc.vector.scalar_tensor_tensor(out=u[:, e, :], in0=u[:, e, :], scalar=col("D", e),
                                                           in1=y_sum[e], op0=ALU.mult, op1=ALU.add)
                        dve.drain()
                        nc.vector.tensor_tensor(gate[:], gate[:], u[:], ALU.mult).then_inc(gated, 1)
                        dve.wait_ge(out_mm, K + 1)
                        dve.wait_ge(recon_stored, K * 16 + 16)
                        if d == 0:
                            nc.vector.tensor_copy(recon[:], flat(0, CB)).then_inc(recon_ready, 1)
                        else:
                            dve.wait_ge(recon_loaded, c * 16 + 16)
                            nc.vector.tensor_tensor(recon[:], loaded[:], flat(0, CB), ALU.add).then_inc(recon_ready, 1)
                            dve.drain()
                            for j in range(CB):
                                nc.vector.bn_stats(stats[:, ds((NCH - 1) * CB + j - c * CB, 1), :],
                                                   recon[:, j * BANK:(j + 1) * BANK])
                        dve.drain()
                        dve.sem_inc(chunk_done, 1)

        FC = 2048
        NF = L // FC
        agg = sb("agg", [128, B, 2])
        dev = sb("dev", [128, B])
        gmean = sb("gmean", [128, B])
        scale = sb("scale", [128, B])
        shift = sb("shift", [128, B])
        std = sb("std", [128, B])
        buf = ring[:, 0:2 * FC].rearrange("p (s n) -> p s n", s=2)
        res = ring[:, 2 * FC:4 * FC].rearrange("p (s n) -> p s n", s=2)
        agg_ready = sem("agg_ready"); gmean_mm = sem("gmean_mm"); dev_ready = sem("dev_ready"); gvar_mm = sem("gvar_mm")
        var_ready = sem("var_ready"); std_ready = sem("std_ready"); affine_ready = sem("affine_ready")
        silu_done = sem("silu_done"); res_done = sem("res_done")
        buf_in = [sem("buf_in_0"), sem("buf_in_1")]; stored = [sem("stored_0"), sem("stored_1")]
        with nc.Block() as block:

            @block.sync
            def _(sp):
                for i in range(2):
                    sp.dma_start(buf[:, i, :], recon_dram[:, i * FC:(i + 1) * FC]).then_inc(buf_in[i], 16)
                for i in range(NF):
                    sp.wait_ge(res_done, i + 1)
                    b, k = i * FC // N, i * FC % N
                    sp.dma_start(out.rearrange("b c h w -> b c (h w)")[b, :, k:k + FC], res[:, i % 2, :])\
                        .then_inc(stored[i % 2], 16)
                    if i + 2 < NF:
                        sp.dma_start(buf[:, i % 2, :], recon_dram[:, (i + 2) * FC:(i + 3) * FC])\
                            .then_inc(buf_in[i % 2], 16)
                for i in range(2):
                    sp.wait_ge(stored[i], 16 * (NF // 2))

            @block.tensor
            def _(pe):
                pe.wait_ge(agg_ready, 1)
                nc.tensor.matmul(ps[:, 0, 0:B], wt("group_mean"), gmean[:], start=True, stop=True).then_inc(gmean_mm, 1)
                pe.wait_ge(dev_ready, 1)
                nc.tensor.matmul(ps[:, 1, 0:B], wt("group_mean"), dev[:], start=True, stop=True).then_inc(gvar_mm, 1)

            @block.scalar
            def _(act):
                act.wait_ge(var_ready, 1)
                nc.scalar.activation(std[:], dev[:], ACT.Sqrt).then_inc(std_ready, 1)
                act.wait_ge(affine_ready, 1)
                for i in range(NF):
                    b = i * FC // N
                    act.wait_ge(buf_in[i % 2], 16 * (i // 2 + 1))
                    if i >= 2:
                        act.wait_ge(stored[i % 2], 16 * (i // 2))
                    nc.scalar.activation(res[:, i % 2, :], buf[:, i % 2, :], ACT.Silu, scale=scale[:, b:b + 1],
                                         bias=shift[:, b:b + 1]).then_inc(silu_done, 1)

            @block.vector
            def _(dve):
                for b in range(B):
                    nc.vector.bn_aggr(agg[:, b, :], stats[:, b * NB:(b + 1) * NB, :])
                dve.drain()
                nc.vector.tensor_copy(gmean[:], agg[:, :, 0]).then_inc(agg_ready, 1)
                dve.wait_ge(gmean_mm, 1)
                nc.vector.tensor_copy(gmean[:], ps[:, 0, 0:B])
                dve.drain()
                nc.vector.tensor_tensor(dev[:], agg[:, :, 0], gmean[:], ALU.subtract)
                dve.drain()
                nc.vector.tensor_tensor(dev[:], dev[:], dev[:], ALU.mult)
                dve.drain()
                nc.vector.tensor_tensor(dev[:], dev[:], agg[:, :, 1], ALU.add).then_inc(dev_ready, 1)
                dve.wait_ge(gvar_mm, 1)
                nc.vector.tensor_scalar(dev[:], ps[:, 1, 0:B], 1e-5, None, ALU.add).then_inc(var_ready, 1)
                dve.wait_ge(std_ready, 1)
                nc.vector.reciprocal(scale[:], std[:])
                dve.drain()
                nc.vector.tensor_scalar(scale[:], scale[:], wt("gn_w"), None, ALU.mult)
                dve.drain()
                nc.vector.tensor_tensor(shift[:], scale[:], gmean[:], ALU.mult)
                dve.drain()
                nc.vector.tensor_scalar(shift[:], shift[:], -1.0, wt("gn_b"), ALU.mult, ALU.add).then_inc(affine_ready, 1)
                for i in range(NF):
                    dve.wait_ge(silu_done, i + 1)
                    nc.vector.tensor_tensor(res[:, i % 2, :], res[:, i % 2, :], xp[:, PAD + i * FC:PAD + (i + 1) * FC],
                                            ALU.add).then_inc(res_done, 1)


def network(nc, x_in, w0, w1, conv1, w2, w3, conv3, select, out):
    with ExitStack() as ctx:
        xp = ctx.enter_context(nc.sbuf_tensor("xp", [128, B * N + 2 * PAD], F32))
        x = xp[:, PAD:PAD + B * N]
        x_loaded = ctx.enter_context(nc.semaphore("x_loaded"))
        with nc.Block() as block:

            @block.sync
            def _(sp):
                sp.dma_start(x.rearrange("c (b n) -> c b n", b=B),
                             x_in.rearrange("b c h w -> c b (h w)")).then_inc(x_loaded, 16)
                sp.wait_ge(x_loaded, 16)

            @block.vector
            def _(dve):
                nc.vector.memset(xp[:, 0:PAD], 0.0)
                nc.vector.memset(xp[:, PAD + B * N:], 0.0)
                dve.drain()

        sparse_attention_layer(nc, x, w0)
        scan_layer(nc, x, w1, conv1, select)
        rank_one_attention_layer(nc, x, w2)
        two_way_scan_layer(nc, xp, w3, conv3, select, out)



def packed(at, width, entries):
    w = _np.zeros((128, width), _np.float32)
    for name, shift, block in entries:
        first = at[name].start + shift
        w[:block.shape[0], first:first + block.shape[1]] = block
    return w


def column(a):
    return a[:, None]


def rows(a, n=128):
    return _np.broadcast_to(a[None, :], (n, a.shape[0]))


def layer0_arrays(q_w, q_b, v_w, v_b, lw1_w, lw1_b, lw2_w, lw2_b, bw1_w, bw1_b, bw2_w, bw2_b, lin_w, lin_b):
    return packed(L0_AT, L0_WIDTH, [
        ("q_w", 0, q_w.T), ("v_w", 0, v_w.T), ("branch_w1", 0, lw1_w.T), ("branch_w1", MID, bw1_w.T),
        ("branch_w2", 0, _np.concatenate([lw2_w.T, _np.zeros((MID, 1))])),
        ("branch_w2", 1, _np.concatenate([_np.zeros((MID, 1)), bw2_w.T])),
        ("lin_w", 0, lin_w.transpose(1, 2, 3, 0).reshape(C, 9 * C)), ("v_b", 0, rows(v_b)), ("q_b", 0, column(q_b)),
        ("branch_b1", 0, column(_np.concatenate([lw1_b, bw1_b]))), ("branch_b2", 0, rows(lw2_b)),
        ("branch_b2", 1, rows(bw2_b)), ("lin_b", 0, column(lin_b)), ("ident", 0, _np.eye(128)),
        ("ones", 0, _np.ones((128, C)))])


def layer1_arrays(W_in, K_conv, b_conv, gamma, beta, W_dt, b_dt, W_dtr, b_dtr, A_log, D_param, W_out):
    w = packed(L1_AT, L1_WIDTH, [
        ("in_w", 0, W_in[:, :C]), ("dt_w", 0, W_dt[:, :R1]), ("bc_w", 0, W_dt[:, R1:]), ("dtr_w", 0, W_dtr),
        ("out_w", 0, W_out), ("ident", 0, _np.eye(128)), ("ones", 0, _np.ones((128, C))), ("A", 0, A_log),
        ("conv_b", 0, column(b_conv)), ("gamma", 0, column(gamma)), ("beta", 0, column(beta)),
        ("dt_b", 0, column(b_dt[:R1])), ("bc_b", 0, column(b_dt[R1:])), ("dtr_b", 0, column(b_dtr)),
        ("D", 0, column(D_param))])
    taps = rows(K_conv[:, 0].transpose(1, 2, 0).reshape(9 * C))
    return w, _np.concatenate([W_in[:, C:], taps], 1)


def layer2_arrays(Wf, bf, Wg, bg, Wh, bh):
    return packed(L2_AT, L2_WIDTH, [("h_w", 0, Wh.T), ("f_w", 0, Wf.T), ("g_w", 0, Wg.T), ("h_b", 0, rows(bh)),
                                    ("f_b", 0, rows(bf)), ("g_b", 0, rows(bg))])


def layer3_arrays(Win, conv_w, conv_b, Wx, Wdt, bdt, A_log, D, Wout, gn_w, gn_b):
    entries = [("u_w", 0, Win[:DI].T), ("z_w", 0, Win[DI:].T), ("dtr_w", 0, Wdt.T), ("gn_w", 0, column(gn_w)),
               ("gn_b", 0, column(gn_b)), ("ident", 0, _np.eye(128))]
    for e in range(TI):
        own = slice(e * 128, (e + 1) * 128)
        for a in range(PARTS):
            entries.append(("bc_w", (e * PARTS + a) * SEL, Wx[R3:, own].T))
        entries += [("dt_w", e * R3, Wx[:R3, own].T), ("out_w", e * 128, Wout[:, own].T), ("A", e * S3, A_log[own]),
                    ("conv_b", e, column(conv_b[own])), ("dtr_b", e, column(bdt[own])), ("D", e, column(D[own]))]
    group_mean = _np.zeros((C, C), _np.float32)
    for first in range(0, C, GROUP):
        group_mean[first:first + GROUP, first:first + GROUP] = 1 / GROUP
    below_top = _np.zeros((128, 2), _np.float32)
    below_top[SEL:3 * SEL, 0] = -1
    below_top[2 * SEL:3 * SEL, 1] = -1
    entries += [("group_mean", 0, group_mean), ("below_top", 0, below_top)]
    return packed(L3_AT, L3_WIDTH, entries), rows(conv_w[:, 0].T.reshape(K3 * DI))


def one_hot_rows():
    select = _np.zeros((PARTS * SEL, SEL, 128), _np.float32)
    for a in range(PARTS):
        for i in range(SEL):
            select[a * SEL + i, i, :] = 1
    return select.reshape(PARTS * SEL, SEL * 128).astype(mybir.dt.np(BF16))


def kernel(**inputs):
    import concourse.bacc as _bacc
    from concourse.bass_utils import run_bass_kernel_spmd as _run

    own = lambda layer: {k[len(layer) + 1:]: _np.asarray(v) for k, v in inputs.items() if k.startswith(layer)}
    w1, conv1 = layer1_arrays(**own("L1_conv"))
    w3, conv3 = layer3_arrays(**own("L3_conv"))
    arrays = {"x_in": _np.asarray(inputs["x"]), "w0": layer0_arrays(**own("L0_conv")), "w1": w1, "conv1": conv1,
              "w2": layer2_arrays(**own("L2_conv")), "w3": w3, "conv3": conv3, "one_hots": one_hot_rows()}
    arrays = {name: _np.ascontiguousarray(a) for name, a in arrays.items()}
    nc = _bacc.Bacc("TRN2", target_bir_lowering=False, num_devices=1)
    args = [nc.dram_tensor(name, a.shape, mybir.dt.from_np(a.dtype), kind="ExternalInput").ap()
            for name, a in arrays.items()]
    out = nc.dram_tensor("out", (B, C, H, W), F32, kind="ExternalOutput").ap()
    network(nc, *args, out)
    result = _run(nc, [arrays], core_ids=[0])
    return result.results[0]["out"]
```

```python
from contextlib import ExitStack

import numpy as _np
import concourse.bass as bass
from concourse import mybir

F32 = mybir.dt.float32
BF16 = mybir.dt.bfloat16
ALU = mybir.AluOpType
ACT = mybir.ActivationFunctionType
AX = mybir.AxisListType

B, C, H, W = 4, 128, 64, 64
N = H * W
T = N // 128
BANK = 512
NB = N // BANK
ds = bass.ds


def columns(widths):
    at, out = 0, {}
    for name, width in widths:
        out[name] = slice(at, at + width)
        at += width
    return out, at


MID = C // 4
L0_WEIGHTS = [("q_w", C), ("v_w", C), ("branch_w1", 2 * MID), ("branch_w2", 2), ("lin_w", 9 * C), ("v_b", C),
              ("q_b", 1), ("branch_b1", 1), ("branch_b2", 2), ("lin_b", 1), ("ident", C), ("ones", C)]
L0_AT, L0_WIDTH = columns(L0_WEIGHTS)


def sparse_attention_layer(nc, x, w, weights_in, first_in, rest_in):
    CH = 1024
    NC = N // CH
    G = N // BANK
    AV_CREDIT = 2 + G
    PE_ORDER = [("logit", 0), ("logit", 1), ("logit", 2), ("transpose", 0), ("logit", 3), ("transpose", 1),
                ("product", 0), ("logit", 4), ("transpose", 2), ("product", 1), ("logit", 5), ("transpose", 3),
                ("product", 2), ("logit", 6), ("transpose", 4), ("product", 3), ("logit", 7), ("transpose", 5),
                ("product", 4), ("transpose", 6), ("product", 5), ("transpose", 7), ("product", 6), ("product", 7)]
    ctx = ExitStack()
    with ctx:
        sb = lambda name, shape, dt=F32: ctx.enter_context(nc.sbuf_tensor("l0_" + name, shape, dt))
        sem = lambda name: ctx.enter_context(nc.semaphore("l0_" + name))
        wt = lambda name: w[:, L0_AT[name]]
        ident, ones = wt("ident"), wt("ones")
        q = sb("q", [128, N])
        k = sb("k", [128, N])
        vT = sb("vT", [128, N])
        E = sb("E", [128, 2, N])
        xb, qsq, hid = E[:, 0, :], E[:, 1, :], E[0:2 * MID, 0, :]
        relu = sb("relu", [128, 2, CH])
        attnT = sb("attnT", [128, 2, BANK])
        y = sb("y", [128, H + 2, W + 2])
        qm = sb("qm", [128, 2, 128])
        sumsq = sb("sumsq", [128, T])
        root = sb("root", [128, T])
        rinv = sb("rinv", [128, T])
        tmp = sb("tmp", [128, T])
        qnorm = sb("qnorm", [128, T])
        wb = sb("wb", [128, 2 * T])
        params = sb("params", [128, T, 2])
        neg_t, neg_max = params[:, :, 0], params[:, :, 1]
        offsets = sb("offsets", [128, 2, 2])
        kpart = sb("kpart", [128, NB])
        kbar = sb("kbar", [128, 1])
        zpart = sb("zpart", [128, 2, NC])
        zsum = sb("zsum", [128, 2])
        zinv = sb("zinv", [128, 2])
        lin = sb("lin", [128, 2, BANK])
        ps = ctx.enter_context(nc.psum_tensor("l0_ps", [128, 8, BANK], F32))
        logits = [ps[:, 0:2, :].rearrange("p a b -> p (a b)"), ps[:, 2:4, :].rearrange("p a b -> p (a b)")]

        banks_free = sem("banks_free")
        x_copied = sem("x_copied")
        q_mm = sem("q_mm"); q_out = sem("q_out"); q_squared = sem("q_squared")
        v_mm = sem("v_mm"); v_out = sem("v_out")
        hid_mm = sem("hid_mm"); hid_out = sem("hid_out"); hid_leaky = sem("hid_leaky")
        stats_mm = sem("stats_mm"); ss_ready = sem("ss_ready"); root_ready = sem("root_ready")
        rinv_ready = sem("rinv_ready"); rinv_mm = sem("rinv_mm"); k_out = sem("k_out")
        kbar_ready = sem("kbar_ready"); mean_mm = sem("mean_mm"); params_ready = sem("params_ready")
        qm_ready = sem("qm_ready"); logits_mm = sem("logits_mm"); relu_ready = sem("relu_ready")
        s_ready = sem("s_ready"); exp_ready = sem("exp_ready"); mask_done = sem("mask_done")
        clip_done = sem("clip_done")
        even_mm = sem("even_mm"); odd_mm = sem("odd_mm"); even_out = sem("even_out"); odd_out = sem("odd_out")
        av_mm = sem("av_mm"); o_out = sem("o_out")
        conv_mm = sem("conv_mm"); lin_out = sem("lin_out"); residual_done = sem("residual_done"); border_zero = sem("border_zero")

        block = ctx.enter_context(nc.Block())

        @block.gpsimd
        def _(pool):
            with pool.Fori(0, B) as b:
                with pool.Fori(0, T // 2) as i:
                    for h in range(2):
                        pool.wait_ge(q_out, b * NB + NB)
                        pool.wait_ge(logits_mm, (b * T + i * 2 + h) * NC + NC)
                        nc.gpsimd.tensor_copy(qm[:, h, :], q[:, ds(i * 256 + h * 128, 128)]).then_inc(qm_ready, 1)

        @block.tensor
        def _(pe):
            pe.sem_inc(logits_mm, 2 * NC)
            pe.sem_inc(av_mm, AV_CREDIT)
            pe.wait_ge(weights_in, 16)
            pe.wait_ge(first_in, 16)
            with pe.Fori(0, B) as b:
                pe.wait_ge(banks_free, b + 1)
                for j in range(NB):
                    nc.tensor.matmul(ps[:, j, :], wt("q_w"), x[:, ds(b * N + j * BANK, BANK)], start=True,
                                     stop=True).then_inc(q_mm, 1)
                pe.wait_ge(x_copied, b + 1)
                for t in range(T):
                    if t % 4 == 0:
                        pe.wait_ge(q_out, b * NB + t // 4 + 1)
                    ins = nc.tensor.matmul(ps[:, t // 4, (t % 4) * 128:(t % 4 + 1) * 128],
                                           xb[:, t * 128:(t + 1) * 128], wt("v_w"), start=True, stop=True)
                    if t % 4 == 3:
                        ins.then_inc(v_mm, 1)
                for j in range(NB):
                    pe.wait_ge(v_out, b * NB + j + 1)
                    nc.tensor.matmul(ps[0:2 * MID, j, :], wt("branch_w1"), q[:, j * BANK:(j + 1) * BANK],
                                     start=True, stop=True).then_inc(hid_mm, 1)
                pe.wait_ge(hid_out, b * NB + NB)
                pe.wait_ge(q_squared, b + 1)
                for t in range(T):
                    nc.tensor.matmul(ps[:, 0, t:t + 1], qsq[:, t * 128:(t + 1) * 128], ones[:, 0:1], start=True,
                                     stop=True)
                pe.wait_ge(hid_leaky, b + 1)
                for t in range(T):
                    ins = nc.tensor.matmul(ps[:, 1, 2 * t:2 * t + 2], hid[:, t * 128:(t + 1) * 128],
                                           w[0:2 * MID, L0_AT["branch_w2"]], start=True, stop=True)
                ins.then_inc(stats_mm, 1)
                pe.wait_ge(rinv_ready, b + 1)
                for t in range(T):
                    ins = nc.tensor.matmul(ps[:, t // 4, (t % 4) * 128:(t % 4 + 1) * 128],
                                           rinv[:, t:t + 1].broadcast_to([128, 128]), ident, start=True, stop=True)
                    if t % 4 == 3:
                        ins.then_inc(rinv_mm, 1)
                pe.wait_ge(kbar_ready, b + 1)
                for t in range(T):
                    ins = nc.tensor.matmul(ps[:, 0, t:t + 1], q[:, t * 128:(t + 1) * 128], kbar[:, 0:1], start=True,
                                           stop=True)
                ins.then_inc(mean_mm, 1)
                pe.wait_ge(params_ready, b + 1)

                def step(new, old, h):
                    def logit(c, j):
                        if c == 0 and j == 0:
                            pe.wait_ge(qm_ready, b * T + new + 1)
                        if j == 0:
                            pe.wait_ge(s_ready, (b * T + new) * NC + c + 1)
                        ins = nc.tensor.matmul(logits[c % 2][:, j * BANK:(j + 1) * BANK], qm[:, h, :],
                                               k[:, c * CH + j * BANK:c * CH + (j + 1) * BANK], start=True,
                                               stop=True)
                        if j == 1:
                            ins.then_inc(logits_mm, 1)

                    def transpose(g):
                        if g % 2 == 0:
                            pe.wait_ge(clip_done, (b * T + old) * NC + g // 2 + 1)
                        pe.wait_ge([even_out, odd_out][g % 2], (b * T + old) * (G // 2) + g // 2 + 1)
                        for j in range(4):
                            at = (4 * g + j) * 128
                            ins = nc.tensor.transpose(ps[:, 4 + g % 2, j * 128:(j + 1) * 128],
                                                      E[:, 1 - h, at:at + 128], ident)
                        ins.then_inc([even_mm, odd_mm][g % 2], 1)

                    def product(g):
                        if g == 0:
                            pe.wait_ge(o_out, b * T + old + 1)
                        pe.wait_ge([even_out, odd_out][g % 2], (b * T + old) * (G // 2) + g // 2 + 2)
                        for j in range(4):
                            t = 4 * g + j
                            ins = nc.tensor.matmul(ps[:, 7 - h, 0:128], vT[:, t * 128:(t + 1) * 128],
                                                   attnT[:, g % 2, j * 128:(j + 1) * 128], start=t == 0,
                                                   stop=t == T - 1)
                        ins.then_inc(av_mm, 1)

                    for work, a in PE_ORDER:
                        if work == "logit" and new is not None:
                            logit(a // 2, a % 2)
                        if work == "transpose" and old is not None:
                            transpose(a)
                        if work == "product" and old is not None:
                            product(a)

                step(0, None, 0)
                with pe.Fori(0, T // 2 - 1) as i:
                    step(i * 2 + 1, i * 2, 1)
                    step(i * 2 + 2, i * 2 + 1, 0)
                step(T - 1, T - 2, 1)
                step(None, T - 1, 0)
                pe.wait_ge(o_out, b * T + T + 2)
                for j in range(NB):
                    for tap in range(9):
                        dy, dx = tap // 3, tap % 3
                        at = L0_AT["lin_w"].start + tap * C
                        ins = nc.tensor.matmul(ps[:, j, :], w[:, at:at + C], y[:, 8 * j + dy:8 * j + dy + 8, dx:dx + W],
                                               start=tap == 0, stop=tap == 8)
                    ins.then_inc(conv_mm, 1)
                pe.wait_ge(rest_in, 16)

        @block.scalar
        def _(act):
            act.sem_inc(even_out, 1)
            act.sem_inc(o_out, 2)
            act.wait_ge(weights_in, 16)
            act.wait_ge(border_zero, 1)
            with act.Fori(0, B) as b:
                for j in range(NB):
                    act.wait_ge(q_mm, b * NB + j + 1)
                    nc.scalar.activation(q[:, j * BANK:(j + 1) * BANK], ps[:, j, :], ACT.Identity,
                                         bias=wt("q_b")).then_inc(q_out, 1)
                for j in range(NB):
                    act.wait_ge(hid_mm, b * NB + j + 1)
                    nc.scalar.activation(hid[:, j * BANK:(j + 1) * BANK], ps[0:2 * MID, j, :], ACT.Identity,
                                         bias=w[0:2 * MID, L0_AT["branch_b1"]]).then_inc(hid_out, 1)
                act.wait_ge(ss_ready, b + 1)
                nc.scalar.activation(root[:], sumsq[:], ACT.Sqrt).then_inc(root_ready, 1)
                act.drain()
                act.wait_ge(params_ready, b + 1)

                def step(new, old, h):
                    def relus(c):
                        act.wait_ge(logits_mm, (b * T + new) * NC + 2 * NC + c + 1)
                        act.wait_ge(mask_done, (b * T + new) * NC + c + 1)
                        nc.scalar.activation(relu[:, c % 2, :], logits[c % 2], ACT.Relu,
                                             bias=offsets[:, h, 0:1]).then_inc(relu_ready, 1)

                    def exps(c):
                        act.wait_ge(s_ready, (b * T + new) * NC + c + 3)
                        part = E[:, h, c * CH:(c + 1) * CH]
                        nc.scalar.activation(part, part, ACT.Exp, bias=offsets[:, h, 1:2],
                                             accum_out=zpart[:, h, c:c + 1]).then_inc(exp_ready, 1)

                    def copy(g):
                        act.wait_ge([even_mm, odd_mm][g % 2], (b * T + old) * (G // 2) + g // 2 + 1)
                        act.wait_ge(av_mm, (b * T + old) * G + g - 1 + AV_CREDIT)
                        nc.scalar.activation(attnT[:, g % 2, :], ps[:, 4 + g % 2, :],
                                             ACT.Copy).then_inc([even_out, odd_out][g % 2], 1)

                    if new is not None:
                        if old is not None:
                            act.drain()
                        nc.scalar.activation(offsets[:, h, :], params[:, ds(new, 1), :].rearrange("p a b -> p (a b)"),
                                             ACT.Copy)
                        act.drain()
                    for work, a in [(relus, 0), (copy, 0), (relus, 1), (exps, 0), (exps, 1), (copy, 2), (relus, 2),
                                    (exps, 2), (copy, 4), (relus, 3), (copy, 5), (exps, 3), (copy, 7)]:
                        if (old if work == copy else new) is not None:
                            work(a)
                    if old is not None:
                        act.wait_ge(av_mm, (b * T + old) * G + G + AV_CREDIT)
                        nc.scalar.activation(y[:, ds(old * 2 + 1, 2), 1:W + 1],
                                             ps[:, 7 - h, 0:128].rearrange("p (a c) -> p a c", a=2),
                                             ACT.Copy).then_inc(o_out, 1)

                step(0, None, 0)
                with act.Fori(0, T // 2 - 1) as i:
                    step(i * 2 + 1, i * 2, 1)
                    step(i * 2 + 2, i * 2 + 1, 0)
                step(T - 1, T - 2, 1)
                step(None, T - 1, 0)
                for j in range(NB):
                    act.wait_ge(conv_mm, b * NB + j + 1)
                    act.wait_ge(residual_done, b * NB + j + 1)
                    nc.scalar.activation(lin[:, j % 2, :], ps[:, j, :], ACT.Identity,
                                         bias=wt("lin_b")).then_inc(lin_out, 1)

        @block.vector
        def _(dve):
            dve.sem_inc(s_ready, 2)
            dve.sem_inc(mask_done, 2)
            dve.sem_inc(odd_out, 1)
            dve.sem_inc(residual_done, 2)
            dve.sem_inc(banks_free, 1)
            nc.vector.memset(y[:], 0.0).then_inc(border_zero, 1)
            dve.wait_ge(weights_in, 16)
            dve.wait_ge(first_in, 16)
            with dve.Fori(0, B) as b:
                nc.vector.tensor_copy(xb, x[:, ds(b * N, N)]).then_inc(x_copied, 1)
                dve.wait_ge(q_out, b * NB + NB)
                nc.vector.tensor_tensor(qsq, q[:], q[:], ALU.mult).then_inc(q_squared, 1)
                for j in range(NB):
                    dve.wait_ge(v_mm, b * NB + j + 1)
                    nc.vector.tensor_tensor(vT[:, j * BANK:(j + 1) * BANK].rearrange("p (a c) -> p a c", a=4),
                                            ps[:, j, :].rearrange("p (a c) -> p a c", a=4),
                                            wt("v_b").unsqueeze(1).broadcast_to([128, 4, 128]),
                                            ALU.add).then_inc(v_out, 1)
                dve.wait_ge(hid_out, b * NB + NB)
                nc.vector.scalar_tensor_tensor(out=hid, in0=hid, scalar=0.2, in1=hid, op0=ALU.mult,
                                               op1=ALU.max).then_inc(hid_leaky, 1)
                dve.wait_ge(stats_mm, b + 1)
                nc.vector.tensor_scalar(sumsq[:], ps[:, 0, 0:T], 1e-8, None, ALU.max).then_inc(ss_ready, 1)
                nc.vector.tensor_copy(wb[:], ps[:, 1, 0:2 * T])
                dve.wait_ge(root_ready, b + 1)
                nc.vector.reciprocal(rinv[:], root[:])
                dve.drain()
                nc.vector.tensor_tensor(tmp[:], sumsq[:], rinv[:], ALU.mult)
                dve.drain()
                nc.vector.tensor_tensor(tmp[:], tmp[:], rinv[:], ALU.mult)
                dve.drain()
                nc.vector.tensor_scalar(tmp[:], tmp[:], -0.5, 1.5, ALU.mult, ALU.add)
                dve.drain()
                nc.vector.tensor_tensor(rinv[:], rinv[:], tmp[:], ALU.mult).then_inc(rinv_ready, 1)
                dve.drain()
                nc.vector.tensor_tensor(qnorm[:], sumsq[:], rinv[:], ALU.mult)
                for j in range(NB):
                    dve.wait_ge(rinv_mm, b * NB + j + 1)
                    nc.vector.scalar_tensor_tensor(out=k[:, j * BANK:(j + 1) * BANK], in0=q[:, j * BANK:(j + 1) * BANK],
                                                   scalar=1.0, in1=ps[:, j, :], op0=ALU.mult, op1=ALU.mult,
                                                   accum_out=kpart[:, j:j + 1])
                dve.drain()
                nc.vector.reduce_sum(kbar[:], kpart[:], axis=AX.X)
                dve.drain()
                nc.vector.tensor_scalar(kbar[:], kbar[:], 1.0 / N, None, ALU.mult).then_inc(kbar_ready, 1)
                nc.vector.tensor_tensor(wb[:].rearrange("p (t a) -> p t a", a=2), wb[:].rearrange("p (t a) -> p t a", a=2),
                                        wt("branch_b2").unsqueeze(1).broadcast_to([128, T, 2]), ALU.add)
                dve.drain()
                dve.wait_ge(mean_mm, b + 1)
                nc.vector.tensor_tensor(tmp[:], wb[:, 0::2], ps[:, 0, 0:T], ALU.mult)
                dve.drain()
                nc.vector.tensor_tensor(neg_t, wb[:, 1::2], tmp[:], ALU.subtract)
                dve.drain()
                nc.vector.tensor_tensor(tmp[:], qnorm[:], neg_t, ALU.add)
                dve.drain()
                nc.vector.tensor_scalar(tmp[:], tmp[:], 0.0, -1.0, ALU.max, ALU.mult)
                dve.drain()
                nc.vector.tensor_tensor(neg_max, tmp[:], qnorm[:], ALU.mult).then_inc(params_ready, 1)

                def step(new, old, h):
                    def exponents(c):
                        if c == 0:
                            dve.wait_ge(av_mm, (b * T + new) * G - G + AV_CREDIT)
                        dve.wait_ge(relu_ready, (b * T + new) * NC + c + 1)
                        nc.vector.tensor_tensor(E[:, h, c * CH:(c + 1) * CH], relu[:, c % 2, :], logits[c % 2],
                                                ALU.mult).then_inc(s_ready, 1)

                    def mask(c):
                        dve.wait_ge(exp_ready, (b * T + new) * NC + c + 1)
                        part = E[:, h, c * CH:(c + 1) * CH]
                        nc.vector.scalar_tensor_tensor(out=part, in0=relu[:, c % 2, :], scalar=0.0, in1=part,
                                                       op0=ALU.is_gt, op1=ALU.mult).then_inc(mask_done, 1)

                    def copy(g):
                        dve.wait_ge([even_mm, odd_mm][g % 2], (b * T + old) * (G // 2) + g // 2 + 1)
                        dve.wait_ge(av_mm, (b * T + old) * G + g - 1 + AV_CREDIT)
                        nc.vector.tensor_copy(attnT[:, g % 2, :],
                                              ps[:, 4 + g % 2, :]).then_inc([even_out, odd_out][g % 2], 1)

                    for work, a in [(exponents, 0), (copy, 1), (exponents, 1), (mask, 0), (mask, 1), (copy, 3),
                                    (exponents, 2), (mask, 2), (exponents, 3), (copy, 6), (mask, 3)]:
                        if (old if work == copy else new) is not None:
                            work(a)
                    if new is not None:
                        nc.vector.reduce_sum(zsum[:, h:h + 1], zpart[:, h, :], axis=AX.X)
                        dve.drain()
                        nc.vector.reciprocal(zinv[:, h:h + 1], zsum[:, h:h + 1])
                        dve.drain()
                        for c in range(NC):
                            part = E[:, h, c * CH:(c + 1) * CH]
                            nc.vector.tensor_scalar(part, part, zinv[:, h:h + 1], 1e-8, ALU.mult,
                                                    ALU.max).then_inc(clip_done, 1)

                step(0, None, 0)
                with dve.Fori(0, T // 2 - 1) as i:
                    step(i * 2 + 1, i * 2, 1)
                    step(i * 2 + 2, i * 2 + 1, 0)
                step(T - 1, T - 2, 1)
                step(None, T - 1, 0)
                for j in range(NB):
                    dve.wait_ge(lin_out, b * NB + j + 1)
                    nc.vector.scalar_tensor_tensor(out=lin[:, j % 2, :], in0=lin[:, j % 2, :], scalar=0.2,
                                                   in1=lin[:, j % 2, :], op0=ALU.mult, op1=ALU.max)
                    dve.drain()
                    part = x[:, ds(b * N + j * BANK, BANK)]
                    nc.vector.tensor_tensor(part, part, lin[:, j % 2, :], ALU.add).then_inc(residual_done, 1)
                dve.wait_ge(rest_in, 16)
                dve.sem_inc(banks_free, 1)


S1 = 64
R1 = 8
L1_WEIGHTS = [("in_w", C), ("dt_w", R1), ("bc_w", 2 * S1), ("dtr_w", C), ("out_w", C), ("ident", C), ("ones", C),
              ("A", S1), ("conv_b", 1), ("gamma", 1), ("beta", 1), ("dt_b", 1), ("bc_b", 1), ("dtr_b", 1), ("D", 1)]
L1_AT, L1_WIDTH = columns(L1_WEIGHTS)
PARTS = 3
SEL = 32


def scan_layer(nc, x, w, sel, weights_in, conv_weights):
    CH = 1024
    NC = N // CH
    CB = CH // BANK
    LAG = 4
    HALF = N // 2
    ctx = ExitStack()
    with ctx:
        sb = lambda name, shape, dt=F32: ctx.enter_context(nc.sbuf_tensor("l1_" + name, shape, dt))
        sem = lambda name: ctx.enter_context(nc.semaphore("l1_" + name))
        wt = lambda name: w[:, L1_AT[name]]
        ident, ones = wt("ident"), wt("ones")
        taps = sb("taps", [128, 9, C])
        stack = sb("stack", [PARTS * SEL, 4, N], BF16)
        delta = sb("delta", [128, N])
        du = sb("du", [128, N])
        g = sb("g", [128, N])
        ring = sb("ring", [128, 10 * CH])
        slots = lambda at, n: ring[:, at * CH:(at + n) * CH].rearrange("p (s n) -> p s n", s=n)
        decay, h, hc, c_row = slots(0, 2), slots(2, 4), slots(6, 2), slots(8, 2)
        u = ring[:, 0:N]
        usq = ring[:, N:2 * N]
        bc = ring[:, N:N + HALF]
        parts = ring[:, N + HALF:N + HALF + PARTS * HALF // 2].bitcast(BF16).rearrange("p (a n) -> p a n", a=PARTS)
        dt_raw = du[0:R1, :]
        QT = N // 4
        soft = [du[:, i * QT:(i + 1) * QT] for i in range(3)]
        conv_raw = delta[:, 0:10 * C]
        carry = sb("carry", [128, S1])
        var = sb("var", [128, T])
        root = sb("root", [128, T])
        rstd = sb("rstd", [128, T])
        tmp = sb("tmp", [128, T])
        row_mean = sb("row_mean", [128, 1])
        ps = ctx.enter_context(nc.psum_tensor("l1_ps", [128, 8, BANK], F32))
        flat = lambda a, n: ps[:, a:a + n, :].rearrange("p a b -> p (a b)")
        b_row = [flat(0, CB), flat(2, CB)]
        c_psum = flat(4, CB)
        y_sum = flat(6, CB)

        conv_in = sem("conv_in"); setup = sem("setup"); taps_ready = sem("taps_ready"); A_ready = sem("A_ready")
        banks_free = sem("banks_free")
        u_mm = sem("u_mm"); u_out = sem("u_out"); squared = sem("squared"); var_mm = sem("var_mm")
        var_ready = sem("var_ready"); root_ready = sem("root_ready"); rstd_ready = sem("rstd_ready")
        rstd_mm = sem("rstd_mm"); u_scaled = sem("u_scaled"); u_ready = sem("u_ready")
        dt_mm = sem("dt_mm"); dt_out = sem("dt_out"); bc_mm = sem("bc_mm"); bc_out = sem("bc_out")
        bc_free = sem("bc_free"); parts_ready = sem("parts_ready"); stack_in = sem("stack_in")
        delta_mm = sem("delta_mm"); delta_out = sem("delta_out"); exp_ready = sem("exp_ready"); ln_ready = sem("ln_ready")
        soft_free = sem("soft_free")
        conv_mm = sem("conv_mm"); silu_out = sem("silu_out"); g_out = sem("g_out"); prep_done = sem("prep_done")
        b_mm = sem("b_mm"); c_mm = sem("c_mm"); c_ready = sem("c_ready"); decay_ready = sem("decay_ready")
        inp_done = sem("inp_done"); scan_done = sem("scan_done"); hc_done = sem("hc_done"); sum_mm = sem("sum_mm")
        y_out = sem("y_out"); out_mm = sem("out_mm")

        block = ctx.enter_context(nc.Block())

        @block.sync
        def _(sp):
            sp.dma_start(conv_raw, conv_weights).then_inc(conv_in, 16)
            with sp.Fori(0, B) as b:
                for hf in range(2):
                    sp.wait_ge(parts_ready, b * 2 + hf + 1)
                    for grp in range(4):
                        for a in range(PARTS):
                            sp.dma_start(stack[a * SEL:(a + 1) * SEL, grp, hf * HALF:(hf + 1) * HALF],
                                         parts[grp * SEL:(grp + 1) * SEL, a, :]).then_inc(stack_in, 16)

        @block.tensor
        def _(pe):
            pe.sem_inc(sum_mm, 2)
            pe.wait_ge(weights_in, 32)
            pe.wait_ge(setup, 1)
            with pe.Fori(0, B) as b:
                pe.wait_ge(banks_free, b + 1)
                for j in range(NB):
                    nc.tensor.matmul(ps[:, j, :], wt("in_w"), x[:, ds(b * N + j * BANK, BANK)], start=True,
                                     stop=True).then_inc(u_mm, 1)
                for t in range(T):
                    if t % (T // 4) == 0:
                        pe.wait_ge(squared, b * 4 + t // (T // 4) + 1)
                    ins = nc.tensor.matmul(ps[:, 0, t:t + 1], usq[:, t * 128:(t + 1) * 128], ones[:, 0:1], start=True,
                                           stop=True)
                ins.then_inc(var_mm, 1)
                pe.wait_ge(rstd_ready, b + 1)
                for t in range(T):
                    ins = nc.tensor.matmul(ps[:, t // 4, (t % 4) * 128:(t % 4 + 1) * 128],
                                           rstd[:, t:t + 1].broadcast_to([128, 128]), ident, start=True, stop=True)
                    if t % 4 == 3:
                        ins.then_inc(rstd_mm, 1)
                for j in range(NB):
                    pe.wait_ge(u_ready, b * NB + j + 1)
                    nc.tensor.matmul(ps[0:R1, j, :], wt("dt_w"), u[:, j * BANK:(j + 1) * BANK], start=True,
                                     stop=True).then_inc(dt_mm, 1)

                def bc_projection(j):
                    nc.tensor.matmul(ps[:, j, :], wt("bc_w"), u[:, j * BANK:(j + 1) * BANK], start=True,
                                     stop=True).then_inc(bc_mm, 1)

                def delta_projection(j):
                    pe.wait_ge(bc_out, b * NB + j + 1)
                    nc.tensor.matmul(ps[:, j, :], w[0:R1, L1_AT["dtr_w"]], dt_raw[:, j * BANK:(j + 1) * BANK],
                                     start=True, stop=True).then_inc(delta_mm, 1)

                def convolution(j):
                    pe.wait_ge(delta_out, b * NB + j + 1)
                    xs = x[:, ds(b * N, N)].rearrange("p (r c) -> p r c", c=W)
                    out = ps[:, j, :].rearrange("p (r c) -> p r c", c=W)
                    order = [(0, 0)] + [(dy, dx) for dy in (-1, 0, 1) for dx in (-1, 0, 1) if (dy, dx) != (0, 0)]
                    for n, (dy, dx) in enumerate(order):
                        r0, r1 = max(8 * j, -dy), min(8 * j + 8, H - dy)
                        c0, c1 = max(0, -dx), min(W, W - dx)
                        ins = nc.tensor.matmul(out[:, r0 - 8 * j:r1 - 8 * j, c0:c1], taps[:, 3 * (dy + 1) + dx + 1, :],
                                               xs[:, r0 + dy:r1 + dy, c0 + dx:c1 + dx], start=n == 0, stop=n == 8)
                    ins.then_inc(conv_mm, 1)

                for j in range(NB):
                    pe.wait_ge(dt_out, b * NB + j + 1)
                    bc_projection(j)
                for j in range(NB // 2):
                    delta_projection(j)
                pe.wait_ge(taps_ready, 1)
                for j in range(2):
                    convolution(j)
                for j in range(NB // 2, NB):
                    delta_projection(j)
                for j in range(2, NB):
                    convolution(j)

                unit = b * NC * S1
                def broadcast_B(c, m, grp, i, s):
                    pe.wait_ge(inp_done, unit + c * S1 + m + 1)
                    for k in range(CB):
                        ins = nc.tensor.matmul(b_row[s][:, k * BANK:(k + 1) * BANK], sel[:, ds(i * 128, 128)],
                                               stack[:, grp, c * CH + k * BANK:c * CH + (k + 1) * BANK], start=True,
                                               stop=True)
                    ins.then_inc(b_mm, 1)

                def broadcast_C(c, m, grp, i):
                    pe.wait_ge(c_ready, unit + c * S1 + m + 1)
                    for k in range(CB):
                        ins = nc.tensor.matmul(c_psum[:, k * BANK:(k + 1) * BANK], sel[:, ds(i * 128, 128)],
                                               stack[:, 2 + grp, c * CH + k * BANK:c * CH + (k + 1) * BANK], start=True,
                                               stop=True)
                    ins.then_inc(c_mm, 1)

                def add_state(c, m, s, start=False, stop=False):
                    pe.wait_ge(hc_done, unit + c * S1 + m + 5)
                    for k in range(CB):
                        ins = nc.tensor.matmul(y_sum[:, k * BANK:(k + 1) * BANK], ident,
                                               hc[:, s, k * BANK:(k + 1) * BANK], start=start, stop=stop)
                    ins.then_inc(sum_mm, 1)

                pe.wait_ge(stack_in, b * (2 * 4 * PARTS * 16) + 2 * 4 * PARTS * 16 + 16)
                pe.wait_ge(g_out, b * NB + NB)
                def last_of_group(c, m):
                    broadcast_C(c, m, m // SEL, SEL - 1)

                for c in range(NC):
                    for m in range(LAG + 2):
                        broadcast_B(c, m, 0, m, m % 2)
                        if m == LAG:
                            pe.wait_ge(y_out, b * NC + c + 1)
                        if m >= LAG:
                            add_state(c, m - LAG, m % 2, start=m == LAG)
                        elif c:
                            add_state(c - 1, S1 - LAG + m, m % 2, stop=m == LAG - 1)
                        if m:
                            broadcast_C(c, m - 1, 0, m - 1)
                        elif c:
                            last_of_group(c - 1, S1 - 1)
                    with pe.Fori(LAG + 2, SEL - 1, 2) as i:
                        for s in range(2):
                            broadcast_B(c, i + s, 0, i + s, s)
                            add_state(c, i + s - LAG, s)
                            broadcast_C(c, i + (s - 1), 0, i + (s - 1))
                    for m in range(SEL, SEL + 2):
                        broadcast_B(c, m, 1, m - SEL, m % 2)
                        add_state(c, m - LAG, m % 2)
                        if m == SEL:
                            last_of_group(c, SEL - 1)
                        else:
                            broadcast_C(c, SEL, 1, 0)
                    with pe.Fori(2, SEL - 1, 2) as i:
                        for s in range(2):
                            broadcast_B(c, i + s + SEL, 1, i + s, s)
                            add_state(c, i + s + (SEL - LAG), s)
                            broadcast_C(c, i + (s - 1) + SEL, 1, i + (s - 1))
                last_of_group(NC - 1, S1 - 1)
                for m in range(LAG):
                    add_state(NC - 1, S1 - LAG + m, m % 2, stop=m == LAG - 1)
                for j in range(NB):
                    if j % CB == 0:
                        pe.wait_ge(y_out, b * NC + j // CB + 2)
                    if j == 0:
                        pe.wait_ge(y_out, b * NC + NC + 1)
                    nc.tensor.matmul(ps[:, j, :], wt("out_w"), g[:, j * BANK:(j + 1) * BANK], start=True,
                                     stop=True).then_inc(out_mm, 1)

        @block.scalar
        def _(act):
            act.sem_inc(c_ready, 1)
            act.wait_ge(weights_in, 32)
            nc.scalar.activation(wt("A"), wt("A"), ACT.Exp).then_inc(A_ready, 1)
            act.wait_ge(setup, 1)
            with act.Fori(0, B) as b:
                for j in range(NB):
                    act.wait_ge(u_mm, b * NB + j + 1)
                    nc.scalar.activation(u[:, j * BANK:(j + 1) * BANK], ps[:, j, :], ACT.Identity).then_inc(u_out, 1)
                act.wait_ge(var_ready, b + 1)
                nc.scalar.activation(root[:], var[:], ACT.Sqrt).then_inc(root_ready, 1)
                for j in range(NB):
                    act.wait_ge(u_scaled, b * NB + j + 1)
                    part = u[:, j * BANK:(j + 1) * BANK]
                    nc.scalar.activation(part, part, ACT.Identity, bias=wt("beta")).then_inc(u_ready, 1)
                for j in range(NB):
                    act.wait_ge(dt_mm, b * NB + j + 1)
                    nc.scalar.activation(dt_raw[:, j * BANK:(j + 1) * BANK], ps[0:R1, j, :], ACT.Identity,
                                         bias=w[0:R1, L1_AT["dt_b"]]).then_inc(dt_out, 1)

                def bc_copy(j):
                    act.wait_ge(bc_mm, b * NB + j + 1)
                    act.wait_ge(bc_free, b * 2 + j // (NB // 2) + 1)
                    nc.scalar.activation(bc[:, j % (NB // 2) * BANK:(j % (NB // 2) + 1) * BANK], ps[:, j, :],
                                         ACT.Identity, bias=wt("bc_b")).then_inc(bc_out, 1)

                act.wait_ge(taps_ready, 1)
                for j in range(2 * NB):
                    half = j // (NB // 2)
                    j = half // 2 * (NB // 2) + j % (NB // 2)
                    if half % 2 == 0:
                        bc_copy(j)
                        continue
                    act.wait_ge(delta_mm, b * NB + j + 1)
                    nc.scalar.activation(delta[:, j * BANK:(j + 1) * BANK], ps[:, j, :], ACT.Identity,
                                         bias=wt("dtr_b")).then_inc(delta_out, 1)
                act.drain()
                for i in range(4):
                    act.wait_ge(soft_free, b * 4 + i + 1)
                    nc.scalar.activation(soft[0], delta[:, i * QT:(i + 1) * QT], ACT.Abs)
                    act.drain()
                    nc.scalar.activation(soft[0], soft[0], ACT.Exp, scale=-1.0).then_inc(exp_ready, 1)
                    act.drain()
                    nc.scalar.activation(soft[1], soft[0], ACT.Ln, bias=1.0).then_inc(ln_ready, 1)
                for j in range(NB):
                    act.wait_ge(conv_mm, b * NB + j + 1)
                    nc.scalar.activation(g[:, j * BANK:(j + 1) * BANK], ps[:, j, :], ACT.Silu,
                                         bias=wt("conv_b")).then_inc(silu_out, 1)
                act.wait_ge(prep_done, b + 1)
                for c in range(NC):
                    with act.Fori(0, S1 - 1, 2) as n:
                        for s in range(2):
                            count = (b * NC + c) * S1 + n + s
                            act.wait_ge(scan_done, count + 1)
                            nc.scalar.activation(decay[:, s, :], delta[:, c * CH:(c + 1) * CH], ACT.Exp,
                                                 scale=wt("A")[:, ds(n + s, 1)]).then_inc(decay_ready, 1)
                            act.wait_ge(c_mm, count + 1)
                            act.wait_ge(hc_done, count + 3)
                            nc.scalar.activation(c_row[:, s, :], c_psum, ACT.Copy).then_inc(c_ready, 1)

        @block.gpsimd
        def _(pool):
            pool.sem_inc(hc_done, 4)
            with pool.Fori(0, B * NC * S1 - 3, 4) as n:
                for s in range(4):
                    pool.wait_ge(c_ready, n + s + 2)
                    pool.wait_ge(scan_done, n + s + 3)
                    pool.wait_ge(sum_mm, n + s + 1)
                    nc.gpsimd.tensor_tensor(hc[:, s % 2, :], h[:, s, :], c_row[:, s % 2, :], ALU.mult).then_inc(hc_done, 1)

        @block.vector
        def _(dve):
            dve.sem_inc(banks_free, 1)
            dve.sem_inc(bc_free, 1)
            dve.sem_inc(soft_free, 1)
            dve.sem_inc(inp_done, 2)
            dve.sem_inc(scan_done, 2)
            dve.sem_inc(y_out, 1)
            dve.sem_inc(stack_in, 16)
            dve.wait_ge(weights_in, 32)
            nc.vector.reduce_sum(row_mean[:], wt("in_w"), axis=AX.X)
            dve.drain()
            nc.vector.tensor_scalar(row_mean[:], row_mean[:], 1.0 / C, None, ALU.mult)
            dve.drain()
            nc.vector.tensor_scalar(wt("in_w"), wt("in_w"), row_mean[:], None, ALU.subtract)
            dve.wait_ge(A_ready, 1)
            nc.vector.tensor_scalar(wt("A"), wt("A"), -1.0, None, ALU.mult).then_inc(setup, 1)
            dve.wait_ge(conv_in, 16)
            nc.vector.tensor_tensor(taps[:], conv_raw[:, C:].rearrange("p (t c) -> p t c", c=C),
                                    conv_raw[:, 0:C].unsqueeze(1).broadcast_to([128, 9, C]), ALU.mult).then_inc(taps_ready, 1)
            with dve.Fori(0, B) as b:
                for i in range(4):
                    dve.wait_ge(u_out, b * NB + (i + 1) * (NB // 4))
                    part = u[:, i * QT:(i + 1) * QT]
                    nc.vector.tensor_tensor(usq[:, i * QT:(i + 1) * QT], part, part, ALU.mult).then_inc(squared, 1)
                dve.wait_ge(var_mm, b + 1)
                nc.vector.tensor_scalar(var[:], ps[:, 0, 0:T], 1.0 / C, 1e-5, ALU.mult, ALU.add).then_inc(var_ready, 1)
                dve.wait_ge(root_ready, b + 1)
                nc.vector.reciprocal(rstd[:], root[:])
                dve.drain()
                nc.vector.tensor_tensor(tmp[:], var[:], rstd[:], ALU.mult)
                dve.drain()
                nc.vector.tensor_tensor(tmp[:], tmp[:], rstd[:], ALU.mult)
                dve.drain()
                nc.vector.tensor_scalar(tmp[:], tmp[:], -0.5, 1.5, ALU.mult, ALU.add)
                dve.drain()
                nc.vector.tensor_tensor(rstd[:], rstd[:], tmp[:], ALU.mult).then_inc(rstd_ready, 1)
                for j in range(NB):
                    dve.wait_ge(rstd_mm, b * NB + j + 1)
                    part = u[:, j * BANK:(j + 1) * BANK]
                    nc.vector.scalar_tensor_tensor(out=part, in0=part, scalar=wt("gamma"), in1=ps[:, j, :],
                                                   op0=ALU.mult, op1=ALU.mult).then_inc(u_scaled, 1)

                def split(hf):
                    dve.wait_ge(bc_out, b * NB + (hf + 1) * (NB // 2))
                    dve.wait_ge(stack_in, (b * 2 + hf) * (4 * PARTS * 16) + 16)
                    for a in range(PARTS):
                        ins = nc.vector.tensor_copy(parts[:, a, :], bc)
                        dve.drain()
                        if a < PARTS - 1:
                            nc.vector.tensor_tensor(bc, bc, parts[:, a, :], ALU.subtract)
                            dve.drain()
                    dve.sem_inc(parts_ready, 1)
                    dve.sem_inc(bc_free, 1)

                nc.vector.memset(carry[:], 0.0)
                split(0)
                split(1)
                for i in range(4):
                    part = delta[:, i * QT:(i + 1) * QT]
                    dve.wait_ge(exp_ready, b * 4 + i + 1)
                    nc.vector.tensor_scalar(soft[2], soft[0], 1.0, 1.0, ALU.add, ALU.subtract)
                    dve.drain()
                    nc.vector.tensor_tensor(soft[2], soft[0], soft[2], ALU.subtract)
                    dve.wait_ge(ln_ready, b * 4 + i + 1)
                    nc.vector.scalar_tensor_tensor(out=part, in0=part, scalar=0.0, in1=soft[1], op0=ALU.max, op1=ALU.add)
                    dve.drain()
                    nc.vector.tensor_tensor(part, part, soft[2], ALU.add).then_inc(soft_free, 1)
                dve.drain()
                nc.vector.tensor_tensor(du[:], delta[:], u, ALU.mult)
                for j in range(NB):
                    part = g[:, j * BANK:(j + 1) * BANK]
                    dve.wait_ge(silu_out, b * NB + j + 1)
                    nc.vector.scalar_tensor_tensor(out=part, in0=ps[:, j, :], scalar=wt("conv_b"), in1=part,
                                                   op0=ALU.add, op1=ALU.mult).then_inc(g_out, 1)
                    dve.drain()
                    nc.vector.scalar_tensor_tensor(out=part, in0=u[:, j * BANK:(j + 1) * BANK], scalar=wt("D"), in1=part,
                                                   op0=ALU.mult, op1=ALU.add)
                dve.drain()
                dve.wait_ge(bc_mm, b * NB + NB)
                dve.sem_inc(prep_done, 1)
                unit = b * NC * S1

                def state_input(c, m, s):
                    dve.wait_ge(b_mm, unit + c * S1 + m + 1)
                    dve.wait_ge(hc_done, unit + c * S1 + m + 1)
                    dve.wait_ge(inp_done, unit + c * S1 + m + 2)
                    nc.vector.tensor_tensor(h[:, s, :], du[:, c * CH:(c + 1) * CH], b_row[s % 2], ALU.mult)\
                        .then_inc(inp_done, 1)

                def scan(c, m, s):
                    dve.wait_ge(inp_done, unit + c * S1 + m + 3)
                    dve.wait_ge(decay_ready, unit + c * S1 + m + 1)
                    nc.vector.tensor_tensor_scan(h[:, s, :], decay[:, s % 2, :], h[:, s, :], carry[:, ds(m, 1)],
                                                 ALU.mult, ALU.add).then_inc(scan_done, 1)

                def keep(c, m, s):
                    dve.wait_ge(scan_done, unit + c * S1 + m + 3)
                    nc.vector.tensor_scalar(carry[:, ds(m, 1)], h[:, s, CH - 1:CH], 1.0, None, ALU.mult)

                def add_y(c):
                    dve.wait_ge(sum_mm, unit + c * S1 + S1 + 2)
                    part = g[:, c * CH:(c + 1) * CH]
                    nc.vector.tensor_tensor(part, part, y_sum, ALU.add).then_inc(y_out, 1)

                for c in range(NC):
                    for m in range(4):
                        state_input(c, m, m)
                        for lag, run in ((1, scan), (2, keep)):
                            if m >= lag:
                                run(c, m - lag, m - lag)
                            elif c:
                                run(c - 1, S1 + m - lag, 4 + m - lag)
                    if c:
                        add_y(c - 1)
                    with dve.Fori(4, S1 - 3, 4) as m:
                        for s in range(4):
                            state_input(c, m + s, s)
                            scan(c, m + s - 1, (s - 1) % 4)
                            keep(c, m + s - 2, (s - 2) % 4)
                scan(NC - 1, S1 - 1, 3)
                add_y(NC - 1)
                for j in range(NB):
                    dve.wait_ge(out_mm, b * NB + j + 1)
                    part = x[:, ds(b * N + j * BANK, BANK)]
                    nc.vector.tensor_tensor(part, part, ps[:, j, :], ALU.add)
                dve.drain()
                dve.sem_inc(banks_free, 1)


L2_WEIGHTS = [("h_w", C), ("f_w", 1), ("g_w", 1), ("h_b", C), ("f_b", 1), ("g_b", 1)]
L2_AT, L2_WIDTH = columns(L2_WEIGHTS)


def rank_one_attention_layer(nc, x, w, weights_in, loads):
    BANK_ORDER = [*range(1, NB), 0]
    ctx = ExitStack()
    with ctx:
        sb = lambda name, shape, dt=F32: ctx.enter_context(nc.sbuf_tensor("l2_" + name, shape, dt))
        sem = lambda name: ctx.enter_context(nc.semaphore("l2_" + name))
        wt = lambda name: w[:, L2_AT[name]]
        xb = sb("xb", [128, N])
        g = sb("g", [128, N])
        hT = sb("hT", [128, N])
        E = sb("E", [128, 2, N])
        hs = sb("hs", [128, 2, C])
        f = sb("f", [128, T])
        neg_max = sb("neg_max", [128, T])
        tmp = sb("tmp", [128, T])
        part_max = sb("part_max", [128, NB])
        part_min = sb("part_min", [128, NB])
        g_max = sb("g_max", [128, 1])
        g_min = sb("g_min", [128, 1])
        zsum = sb("zsum", [128, 2])
        zinv = sb("zinv", [128, 2])
        ps = ctx.enter_context(nc.psum_tensor("l2_ps", [128, 8, BANK], F32))

        xb_ready = sem("xb_ready"); bank_free = sem("bank_free")
        g_mm = sem("g_mm"); g_out = sem("g_out"); f_mm = sem("f_mm"); f_out = sem("f_out")
        h_mm = sem("h_mm"); h_out = sem("h_out"); max_ready = sem("max_ready")
        exp_ready = sem("exp_ready"); hs_ready = sem("hs_ready"); tile_mm = sem("tile_mm"); sum_mm = sem("sum_mm")

        block = ctx.enter_context(nc.Block())

        @block.sync
        def _(sp):
            for to, at, signal in loads:
                sp.dma_start(to, at).then_inc(signal, 16)

        @block.tensor
        def _(pe):
            pe.sem_inc(tile_mm, 2)
            pe.wait_ge(weights_in, 16)
            with pe.Fori(0, B) as b:
                for j in BANK_ORDER:
                    pe.wait_ge(bank_free, b * NB + j + 1)
                    if j == 0:
                        pe.wait_ge(xb_ready, b + 1)
                        for t in range(T):
                            ins = nc.tensor.matmul(ps[:, 0, t:t + 1], xb[:, t * 128:(t + 1) * 128], wt("f_w"),
                                                   start=True, stop=True)
                        ins.then_inc(f_mm, 1)
                        pe.wait_ge(f_out, b + 1)
                    nc.tensor.matmul(ps[:, j, :], wt("g_w").broadcast_to([128, 128]),
                                     x[:, ds(b * N + j * BANK, BANK)], start=True, stop=True).then_inc(g_mm, 1)
                for n, j in enumerate(BANK_ORDER):
                    pe.wait_ge(g_out, b * NB + n + 1)
                    for a in range(4):
                        t = 4 * j + a
                        ins = nc.tensor.matmul(ps[:, j, a * 128:(a + 1) * 128], xb[:, t * 128:(t + 1) * 128],
                                               wt("h_w"), start=True, stop=True)
                    ins.then_inc(h_mm, 1)
                pe.wait_ge(h_out, b * NB + NB)

                def tile(t, s, start=False, stop=False):
                    pe.wait_ge(hs_ready, b * T + t + 1)
                    for j in range(NB):
                        ins = nc.tensor.matmul(ps[:, j, :], hs[:, s, :], E[:, s, j * BANK:(j + 1) * BANK], start=start,
                                               stop=stop)
                        if stop:
                            ins.then_inc(sum_mm, 1)
                    if not stop:
                        ins.then_inc(tile_mm, 1)

                tile(0, 0, start=True)
                with pe.Fori(1, T - 2, 2) as t:
                    tile(t, 1)
                    tile(t + 1, 0)
                tile(T - 1, 1, stop=True)
                pe.wait_ge(sum_mm, b * NB + NB)
                pe.sem_inc(tile_mm, 1)

        @block.scalar
        def _(act):
            act.wait_ge(weights_in, 16)
            with act.Fori(0, B) as b:
                for n, j in enumerate(BANK_ORDER):
                    act.wait_ge(g_mm, b * NB + n + 1)
                    nc.scalar.activation(g[:, j * BANK:(j + 1) * BANK], ps[:, j, :], ACT.Identity,
                                         bias=wt("g_b")).then_inc(g_out, 1)
                act.wait_ge(max_ready, b + 1)
                with act.Fori(0, T - 1, 2) as t:
                    for s in range(2):
                        act.wait_ge(tile_mm, b * T + t + s + 1)
                        nc.scalar.activation(E[:, s, :], g[:], ACT.Exp, scale=f[:, ds(t + s, 1)],
                                             bias=neg_max[:, ds(t + s, 1)],
                                             accum_out=zsum[:, s:s + 1]).then_inc(exp_ready, 1)

        @block.vector
        def _(dve):
            dve.sem_inc(bank_free, NB)
            dve.wait_ge(weights_in, 16)
            with dve.Fori(0, B) as b:
                nc.vector.tensor_copy(xb[:], x[:, ds(b * N, N)]).then_inc(xb_ready, 1)
                for n, j in enumerate(BANK_ORDER):
                    if j == 0:
                        dve.wait_ge(f_mm, b + 1)
                        nc.vector.tensor_scalar(f[:], ps[:, 0, 0:T], wt("f_b"), None, ALU.add).then_inc(f_out, 1)
                    dve.wait_ge(g_out, b * NB + n + 1)
                    part = g[:, j * BANK:(j + 1) * BANK]
                    nc.vector.reduce_max(part_max[:, n:n + 1], part, axis=AX.X)
                    nc.vector.tensor_reduce(part_min[:, n:n + 1], part, AX.X, ALU.min)
                dve.drain()
                nc.vector.reduce_max(g_max[:], part_max[:], axis=AX.X)
                nc.vector.tensor_reduce(g_min[:], part_min[:], AX.X, ALU.min)
                dve.drain()
                nc.vector.tensor_scalar(neg_max[:], f[:], g_max[:], None, ALU.mult)
                nc.vector.tensor_scalar(tmp[:], f[:], g_min[:], None, ALU.mult)
                dve.drain()
                nc.vector.tensor_tensor(neg_max[:], neg_max[:], tmp[:], ALU.max)
                dve.drain()
                nc.vector.tensor_scalar(neg_max[:], neg_max[:], -1.0, None, ALU.mult).then_inc(max_ready, 1)
                for n, j in enumerate(BANK_ORDER):
                    dve.wait_ge(h_mm, b * NB + n + 1)
                    nc.vector.tensor_tensor(hT[:, j * BANK:(j + 1) * BANK].rearrange("p (a c) -> p a c", a=4),
                                            ps[:, j, :].rearrange("p (a c) -> p a c", a=4),
                                            wt("h_b").unsqueeze(1).broadcast_to([128, 4, C]), ALU.add).then_inc(h_out, 1)
                with dve.Fori(0, T - 1, 2) as t:
                    for s in range(2):
                        dve.wait_ge(exp_ready, b * T + t + s + 1)
                        nc.vector.reciprocal(zinv[:, s:s + 1], zsum[:, s:s + 1])
                        dve.drain()
                        nc.vector.tensor_scalar(hs[:, s, :], hT[:, ds((t + s) * C, C)], zinv[:, s:s + 1], None,
                                                ALU.mult).then_inc(hs_ready, 1)
                for j in range(NB):
                    dve.wait_ge(sum_mm, b * NB + j + 1)
                    part = x[:, ds(b * N + j * BANK, BANK)]
                    nc.vector.tensor_tensor(part, part, ps[:, j, :], ALU.add).then_inc(bank_free, 1)
                dve.drain()


DI = 256
TI = DI // 128
S3 = 16
R3 = 8
K3 = 4
PAD = K3 - 1
GROUP = 32
DT_AT = PARTS * SEL
L3_WEIGHTS = [("u_w", DI), ("z_w", DI), ("bc_w", TI * (DT_AT + R3)), ("dtr_w", DI), ("out_w", DI), ("ident", C),
              ("A", TI * S3), ("conv_b", TI), ("dtr_b", TI), ("D", TI), ("gn_w", 1), ("gn_b", 1),
              ("group_mean", C), ("below_top", 2)]
L3_AT, L3_WIDTH = columns(L3_WEIGHTS)


def two_way_scan_layer(nc, xp, w, conv_rows, sel, weights_in, out):
    L = B * N
    CH = BANK
    NCH = L // CH
    UNITS = S3 * TI
    LAG = 3
    AHEAD = 2
    DS = 8
    N_BC, N_DELTA = 7, 10
    ctx = ExitStack()
    with ctx:
        sb = lambda name, shape, dt=F32: ctx.enter_context(nc.sbuf_tensor("l3_" + name, shape, dt))
        sem = lambda name: ctx.enter_context(nc.semaphore("l3_" + name))
        recon_dram = nc.dram_tensor("l3_recon_dram", [128, L], F32, kind="Internal").ap()
        wt = lambda name: w[:, L3_AT[name]]
        ident = wt("ident")
        col = lambda name, i, n=1: w[:, L3_AT[name].start + i:L3_AT[name].start + i + n]
        taps = sb("taps", [128, K3, DI])
        ring = sb("ring", [128, 24 * CH])
        slots = lambda at, n: ring[:, at * CH:(at + n) * CH].rearrange("p (s n) -> p s n", s=n)
        decay, h, hc, c_row = slots(0, DS), slots(DS, 8), slots(16, 4), slots(20, 4)
        u = sb("u", [128, 2, TI, CH])
        gate = sb("gate", [128, 2, TI, CH])
        delta = sb("delta", [128, 2, TI, CH])
        du = sb("du", [128, 2, TI, CH])
        stack = sb("stack", [PARTS * SEL, 2, CH], BF16)
        z1, z2, z3 = (sb(f"z{i}", [128, TI, CH]) for i in (1, 2, 3))
        gated = sb("gated", [128, TI, CH])
        dt_raw = sb("dt_raw", [128, CH])[DT_AT:DT_AT + R3, :]
        rest = sb("rest", [PARTS * SEL, CH])
        part = sb("part", [PARTS * SEL, CH], BF16)
        recon = sb("recon", [128, CH])
        loaded = sb("loaded", [128, CH])
        carry = sb("carry", [128, UNITS])
        stats = sb("stats", [128, L // BANK, 6])
        ps = ctx.enter_context(nc.psum_tensor("l3_ps", [128, 8, BANK], F32))
        b_psum, c_psum, y_sum = ps[:, 0:2, :], ps[:, 2:4, :], ps[:, 4:6, :]
        even, odd = ps[:, 6, :], ps[:, 7, :]

        setup = sem("setup"); A_ready = sem("A_ready")
        u_mm = sem("u_mm"); u_out = sem("u_out"); z_mm = sem("z_mm"); gate_out = sem("gate_out")
        bc_mm = sem("bc_mm"); dt_out = sem("dt_out"); high = sem("high"); rest_ready = sem("rest_ready")
        middle = sem("middle"); stack_ready = sem("stack_ready")
        delta_mm = sem("delta_mm"); delta_out = sem("delta_out"); exp_ready = sem("exp_ready"); ln_ready = sem("ln_ready")
        delta_ready = sem("delta_ready"); du_ready = sem("du_ready")
        b_mm = sem("b_mm"); c_mm = sem("c_mm"); c_ready = sem("c_ready"); decay_ready = sem("decay_ready")
        inp_done = sem("inp_done"); scan_done = sem("scan_done"); hc_done = sem("hc_done"); sum_mm = sem("sum_mm")
        y_out = sem("y_out"); gated_ready = sem("gated_ready"); out_mm = sem("out_mm"); recon_ready = sem("recon_ready")
        recon_stored = sem("recon_stored"); recon_loaded = sem("recon_loaded"); loaded_used = sem("loaded_used")

        def chunks(engine, body):
            for d in range(2):
                first = d * NCH
                body(first, 0, d, 0, d - 1 if d else None, (d, 1), (d, 2))
                with engine.Fori(0, NCH // 2 - 2) as i:
                    body(i * 2 + (first + 1), 1, d, i * 2 + 1, d, (d, i * 2 + 2), (d, i * 2 + 3))
                    body(i * 2 + (first + 2), 0, d, i * 2 + 2, d, (d, i * 2 + 3), (d, i * 2 + 4))
                turn = (lambda n: (1, n)) if d == 0 else (lambda n: None)
                body(first + NCH - 3, 1, d, NCH - 3, d, (d, NCH - 2), (d, NCH - 1))
                body(first + NCH - 2, 0, d, NCH - 2, d, (d, NCH - 1), turn(0))
                body(first + NCH - 1, 1, d, NCH - 1, d, turn(0), turn(1))

        with nc.Block() as block:

            @block.sync
            def _(sp):
                with sp.Fori(0, NCH) as c:
                    sp.wait_ge(recon_ready, c + 2)
                    sp.dma_start(recon_dram[:, ds(c * CH, CH)], recon[:]).then_inc(recon_stored, 16)
                sp.wait_ge(recon_stored, 16 * NCH + 16)
                with sp.Fori(0, NCH) as c:
                    sp.wait_ge(loaded_used, c + 1)
                    sp.dma_start(loaded[:], recon_dram[:, ds((c - (NCH - 1)) * -CH, CH)]).then_inc(recon_loaded, 16)
                    sp.wait_ge(recon_ready, c + (NCH + 2))
                    sp.dma_start(recon_dram[:, ds((c - (NCH - 1)) * -CH, CH)], recon[:]).then_inc(recon_stored, 16)
                sp.wait_ge(recon_stored, 2 * 16 * NCH + 16)

            @block.tensor
            def _(pe):
                def prep_u(K, d, c, e, some=range(K3)):
                    at = (c - (NCH - 1)) * -CH if d else c * CH
                    if 0 in some:
                        pe.wait_ge(delta_out, K * TI + e + 1)
                    for k in some:
                        shift = PAD - k if d else k - PAD
                        ins = nc.tensor.matmul([even, odd][e], taps[:, k, e * 128:(e + 1) * 128],
                                               xp[:, ds(at + (PAD + shift), CH)], start=k == 0, stop=k == K3 - 1)
                    if K3 - 1 in some:
                        ins.then_inc(u_mm, 1)

                def prep_z(K, d, c):
                    at = (c - (NCH - 1)) * -CH if d else c * CH
                    for e in range(TI):
                        pe.wait_ge(u_out, K * TI + e + 1)
                        nc.tensor.matmul([even, odd][e], col("z_w", e * 128, 128), xp[:, ds(at + PAD, CH)], start=True,
                                         stop=True).then_inc(z_mm, 1)

                def prep_bc(K, p):
                    pe.wait_ge(gate_out, K * TI + TI)
                    for e in range(TI):
                        ins = nc.tensor.matmul(odd[0:DT_AT + R3, :], col("bc_w", e * (DT_AT + R3), DT_AT + R3),
                                               u[:, p, e, :], start=e == 0, stop=e == TI - 1)
                    ins.then_inc(bc_mm, 1)

                def prep_delta(K):
                    pe.wait_ge(dt_out, K + 1)
                    for e in range(TI):
                        if e == 0:
                            if not isinstance(K, int) or K:
                                pe.wait_ge(recon_ready, K)
                        else:
                            pe.wait_ge(rest_ready, K + 1)
                        nc.tensor.matmul([even, odd][e],
                                         w[DT_AT:DT_AT + R3, L3_AT["dtr_w"].start + e * 128:L3_AT["dtr_w"].start + (e + 1) * 128],
                                         dt_raw, start=True, stop=True).then_inc(delta_mm, 1)

                def broadcasts(K, n, p):
                    if n == 0:
                        pe.wait_ge(stack_ready, K + 1)
                    pe.wait_ge(inp_done, K * UNITS + (n * TI + 2))
                    nc.tensor.matmul(b_psum[:, n % 2, :], sel[:, n * 128:(n + 1) * 128], stack[:, p, :], start=True,
                                     stop=True).then_inc(b_mm, 1)
                    pe.wait_ge(c_ready, K * S3 + (n + 1))
                    nc.tensor.matmul(c_psum[:, n % 2, :], sel[:, (S3 + n) * 128:(S3 + n + 1) * 128], stack[:, p, :],
                                     start=True, stop=True).then_inc(c_mm, 1)

                def add_state(K, n):
                    if n == 0:
                        pe.wait_ge(y_out, K + 1)
                    for e in range(TI):
                        pe.wait_ge(hc_done, K * UNITS + (n * TI + e + 9))
                        nc.tensor.matmul(y_sum[:, e, :], ident, hc[:, (n * TI + e) % 4, :], start=n == 0,
                                         stop=n == S3 - 1).then_inc(sum_mm, 1)

                def project(K):
                    pe.wait_ge(gated_ready, K + 2)
                    for e in range(TI):
                        ins = nc.tensor.matmul(even, col("out_w", e * 128, 128), gated[:, e, :], start=e == 0,
                                               stop=e == TI - 1)
                    ins.then_inc(out_mm, 1)

                def body(K, p, d, c, prev_d, after, later):
                    for n in range(S3):
                        broadcasts(K, n, p)
                        if n >= LAG:
                            add_state(K, n - LAG)
                        elif prev_d is not None:
                            add_state(K - 1, S3 + n - LAG)
                        if after is not None:
                            if n < K3:
                                prep_u(K + 1, *after, 1, [n])
                            if n == 4:
                                prep_z(K + 1, *after)
                            if n == N_BC:
                                prep_bc(K + 1, 1 - p)
                            if n == N_DELTA:
                                prep_delta(K + 1)
                        if n >= S3 - K3 and later is not None:
                            prep_u(K + 2, *later, 0, [n - (S3 - K3)])
                        if n == 5 and prev_d is not None:
                            if after is not None:
                                pe.wait_ge(gate_out, (K + 1) * TI + 1)
                            project(K - 1)

                pe.sem_inc(sum_mm, 4)
                pe.wait_ge(weights_in, 32)
                pe.wait_ge(setup, 1)
                for e in range(TI):
                    prep_u(0, 0, 0, e)
                prep_z(0, 0, 0)
                prep_bc(0, 0)
                prep_delta(0)
                prep_u(1, 0, 1, 0)
                chunks(pe, body)
                for n in range(S3 - LAG, S3):
                    add_state(2 * NCH - 1, n)
                project(2 * NCH - 1)

            @block.scalar
            def _(act):
                def silus(K, p):
                    for e in range(TI):
                        act.wait_ge(u_mm, K * TI + e + 1)
                        if not isinstance(K, int) or K:
                            act.wait_ge(gated_ready, K)
                        nc.scalar.activation(u[:, p, e, :], [even, odd][e], ACT.Silu,
                                             bias=col("conv_b", e)).then_inc(u_out, 1)
                    for e in range(TI):
                        act.wait_ge(z_mm, K * TI + e + 1)
                        nc.scalar.activation(gate[:, p, e, :], [even, odd][e], ACT.Silu).then_inc(gate_out, 1)

                def splits(K):
                    act.wait_ge(bc_mm, K + 1)
                    nc.scalar.activation(part[:], odd[0:PARTS * SEL, :], ACT.Copy).then_inc(high, 1)
                    nc.scalar.activation(dt_raw, odd[DT_AT:DT_AT + R3, :], ACT.Copy).then_inc(dt_out, 1)

                def split_again(K):
                    act.wait_ge(rest_ready, K + 1)
                    nc.scalar.activation(part[:], rest[:], ACT.Copy).then_inc(middle, 1)

                def deltas(K, p):
                    for e in range(TI):
                        act.wait_ge(delta_mm, K * TI + e + 1)
                        nc.scalar.activation(delta[:, p, e, :], [even, odd][e], ACT.Identity,
                                             bias=col("dtr_b", e)).then_inc(delta_out, 1)
                    act.drain()
                    nc.scalar.activation(z1[:], delta[:, p, :, :], ACT.Abs)
                    act.drain()
                    nc.scalar.activation(z1[:], z1[:], ACT.Exp, scale=-1.0).then_inc(exp_ready, 1)

                def logs():
                    act.drain()
                    nc.scalar.activation(z2[:], z1[:], ACT.Ln, bias=1.0).then_inc(ln_ready, 1)

                def decays(K, n, p):
                    if n == 0:
                        act.wait_ge(delta_ready, K + 1)
                    for e in range(TI):
                        s = n * TI + e
                        act.wait_ge(scan_done, K * UNITS + (s + 1))
                        nc.scalar.activation(decay[:, s % DS, :], delta[:, p, e, :], ACT.Exp,
                                             scale=col("A", e * S3 + n)).then_inc(decay_ready, 1)

                def c_copy(K, n):
                    act.wait_ge(c_mm, K * S3 + (n + 1))
                    act.wait_ge(hc_done, K * UNITS + (n * TI + 2))
                    nc.scalar.activation(c_row[:, n % 4, :], c_psum[:, n % 2, :], ACT.Copy).then_inc(c_ready, 1)

                def body(K, p, d, c, prev_d, after, later):
                    for n in range(S3):
                        c_copy(K, n)
                        if n + AHEAD < S3:
                            decays(K, n + AHEAD, p)
                        elif after is not None:
                            decays(K + 1, n + AHEAD - S3, 1 - p)
                        if after is not None:
                            if n == 3:
                                silus(K + 1, 1 - p)
                            if n == N_BC:
                                splits(K + 1)
                            if n == N_BC + 1:
                                split_again(K + 1)
                            if n == N_DELTA:
                                deltas(K + 1, 1 - p)
                            if n == N_DELTA + 1:
                                logs()

                act.sem_inc(c_ready, 2)
                act.sem_inc(delta_out, TI)
                act.wait_ge(weights_in, 32)
                nc.scalar.activation(wt("A"), wt("A"), ACT.Exp).then_inc(A_ready, 1)
                act.wait_ge(setup, 1)
                silus(0, 0)
                splits(0)
                split_again(0)
                deltas(0, 0)
                logs()
                for n in range(AHEAD):
                    decays(0, n, 0)
                chunks(act, body)

            @block.gpsimd
            def _(pool):
                def input_rate(K, p):
                    pool.wait_ge(delta_ready, K + 1)
                    nc.gpsimd.tensor_tensor(du[:, p, :, :], delta[:, p, :, :], u[:, p, :, :], ALU.mult).then_inc(du_ready, 1)

                def body(K, p, d, c, prev_d, after, later):
                    last = 0 if d else CH - 1
                    for n in range(S3):
                        for e in range(TI):
                            s = n * TI + e
                            if e == 0:
                                pool.wait_ge(c_ready, K * S3 + (n + 3))
                            pool.wait_ge(sum_mm, K * UNITS + (s + 1))
                            pool.wait_ge(scan_done, K * UNITS + (s + 1 + DS))
                            ins = nc.gpsimd.tensor_tensor(hc[:, s % 4, :], h[:, s % 8, :], c_row[:, n % 4, :], ALU.mult)
                            if after is not None and after[0] == d:
                                ins = nc.gpsimd.tensor_scalar(carry[:, s:s + 1], h[:, s % 8, last:last + 1], 1.0, None,
                                                              ALU.mult)
                            ins.then_inc(hc_done, 1)
                        if n == 13 and after is not None:
                            input_rate(K + 1, 1 - p)

                pool.sem_inc(hc_done, 8)
                input_rate(0, 0)
                chunks(pool, body)

            @block.vector
            def _(dve):
                def split_rest(K):
                    dve.wait_ge(high, K + 1)
                    nc.vector.scalar_tensor_tensor(out=rest[:], in0=part[:], scalar=col("below_top", 0)[0:PARTS * SEL, :],
                                                   in1=odd[0:PARTS * SEL, :], op0=ALU.mult,
                                                   op1=ALU.add).then_inc(rest_ready, 1)

                def split_last(K, p):
                    dve.wait_ge(middle, K + 1)
                    nc.vector.scalar_tensor_tensor(out=stack[:, p, :], in0=part[:],
                                                   scalar=col("below_top", 1)[0:PARTS * SEL, :], in1=rest[:],
                                                   op0=ALU.mult, op1=ALU.add).then_inc(stack_ready, 1)

                def soft_a(K):
                    dve.wait_ge(exp_ready, K + 1)
                    nc.vector.tensor_scalar(z3[:], z1[:], 1.0, 1.0, ALU.add, ALU.subtract)

                def soft_b(K):
                    dve.drain()
                    nc.vector.tensor_tensor(z3[:], z1[:], z3[:], ALU.subtract)

                def soft_c(K, p):
                    dve.wait_ge(ln_ready, K + 1)
                    part_d = delta[:, p, :, :]
                    nc.vector.scalar_tensor_tensor(out=part_d, in0=part_d, scalar=0.0, in1=z2[:], op0=ALU.max, op1=ALU.add)

                def soft_d(K, p):
                    dve.drain()
                    part_d = delta[:, p, :, :]
                    nc.vector.tensor_tensor(part_d, part_d, z3[:], ALU.add).then_inc(delta_ready, 1)

                def state_input(K, s, p):
                    if s == 0:
                        dve.wait_ge(du_ready, K + 1)
                    if s % TI == 0:
                        dve.wait_ge(b_mm, K * S3 + (s // TI + 1))
                    dve.wait_ge(hc_done, K * UNITS + (s + 1))
                    nc.vector.tensor_tensor(h[:, s % 8, :], du[:, p, s % TI, :], b_psum[:, s // TI % 2, :], ALU.mult)\
                        .then_inc(inp_done, 1)

                def scan(K, s, d):
                    order = slice(None, None, -1) if d else slice(None)
                    dve.wait_ge(inp_done, K * UNITS + (s + 5))
                    dve.wait_ge(decay_ready, K * UNITS + (s + 1))
                    nc.vector.tensor_tensor_scan(h[:, s % 8, order], decay[:, s % DS, order], h[:, s % 8, order],
                                                 carry[:, s:s + 1], ALU.mult, ALU.add).then_inc(scan_done, 1)

                def gating(K, p):
                    dve.wait_ge(sum_mm, K * UNITS + (UNITS + 4))
                    dve.wait_ge(out_mm, K + 1)
                    for e in range(TI):
                        ins = nc.vector.scalar_tensor_tensor(out=gated[:, e, :], in0=u[:, p, e, :], scalar=col("D", e),
                                                             in1=y_sum[:, e, :], op0=ALU.mult, op1=ALU.add)
                    ins.then_inc(y_out, 1)
                    dve.drain()
                    nc.vector.tensor_tensor(gated[:], gated[:], gate[:, p, :, :], ALU.mult).then_inc(gated_ready, 1)

                def result(K, d, c):
                    dve.wait_ge(out_mm, K + 2)
                    dve.wait_ge(recon_stored, K * 16 + 16)
                    if d == 0:
                        nc.vector.tensor_copy(recon[:], even).then_inc(recon_ready, 1)
                    else:
                        dve.wait_ge(recon_loaded, (K - NCH) * 16 + 16)
                        nc.vector.tensor_tensor(recon[:], loaded[:], even, ALU.add).then_inc(recon_ready, 1)
                        dve.drain()
                        nc.vector.bn_stats(stats[:, ds((K - (2 * NCH - 1)) * -1, 1), :], recon[:])
                        dve.sem_inc(loaded_used, 1)

                def body(K, p, d, c, prev_d, after, later):
                    for s in range(UNITS):
                        state_input(K, s, p)
                        if s:
                            scan(K, s - 1, d)
                        elif prev_d is not None:
                            scan(K - 1, UNITS - 1, prev_d)
                        if s == 0 and prev_d is not None and prev_d != d:
                            dve.drain()
                            nc.vector.memset(carry[:], 0.0)
                            dve.drain()
                        if prev_d is not None:
                            if s == 4:
                                gating(K - 1, 1 - p)
                            if s == 13:
                                result(K - 1, prev_d, c)
                        if after is not None:
                            if s == 2 * N_BC + 2:
                                split_rest(K + 1)
                            if s == 2 * N_BC + 5:
                                split_last(K + 1, 1 - p)
                            if s == 2 * N_DELTA + 4:
                                soft_a(K + 1)
                            if s == 2 * N_DELTA + 5:
                                soft_b(K + 1)
                            if s == 2 * N_DELTA + 7:
                                soft_c(K + 1, 1 - p)
                            if s == 2 * N_DELTA + 8:
                                soft_d(K + 1, 1 - p)

                dve.sem_inc(inp_done, 4)
                dve.sem_inc(scan_done, DS)
                dve.sem_inc(y_out, 1)
                dve.sem_inc(gated_ready, 1)
                dve.sem_inc(recon_ready, 1)
                dve.sem_inc(out_mm, 1)
                dve.sem_inc(loaded_used, 1)
                dve.sem_inc(recon_stored, 16)
                dve.wait_ge(weights_in, 32)
                for k in range(K3):
                    nc.vector.tensor_tensor(taps[:, k, :], conv_rows[:, k * DI:(k + 1) * DI], wt("u_w"), ALU.mult)
                nc.vector.memset(carry[:], 0.0)
                dve.wait_ge(A_ready, 1)
                nc.vector.tensor_scalar(wt("A"), wt("A"), -1.0, None, ALU.mult).then_inc(setup, 1)
                split_rest(0)
                split_last(0, 0)
                soft_a(0)
                soft_b(0)
                soft_c(0, 0)
                soft_d(0, 0)
                chunks(dve, body)
                last = 2 * NCH - 1
                scan(last, UNITS - 1, 1)
                gating(last, 1)
                result(last, 1, None)

        FC = 2048
        NF = L // FC
        agg = sb("agg", [128, B, 2])
        dev = sb("dev", [128, B])
        gmean = sb("gmean", [128, B])
        scale = sb("scale", [128, B])
        shift = sb("shift", [128, B])
        std = sb("std", [128, B])
        buf = ring[:, 0:2 * FC].rearrange("p (s n) -> p s n", s=2)
        res = ring[:, 2 * FC:4 * FC].rearrange("p (s n) -> p s n", s=2)
        agg_ready = sem("agg_ready"); gmean_mm = sem("gmean_mm"); dev_ready = sem("dev_ready"); gvar_mm = sem("gvar_mm")
        var_ready = sem("var_ready"); std_ready = sem("std_ready"); affine_ready = sem("affine_ready")
        silu_done = sem("silu_done"); res_done = sem("res_done")
        buf_in = [sem("buf_in_0"), sem("buf_in_1")]; stored = [sem("stored_0"), sem("stored_1")]
        with nc.Block() as block:

            @block.sync
            def _(sp):
                for i in range(2):
                    sp.dma_start(buf[:, i, :], recon_dram[:, i * FC:(i + 1) * FC]).then_inc(buf_in[i], 16)
                for i in range(NF):
                    sp.wait_ge(res_done, i + 1)
                    b, k = i * FC // N, i * FC % N
                    sp.dma_start(out.rearrange("b c h w -> b c (h w)")[b, :, k:k + FC], res[:, i % 2, :])\
                        .then_inc(stored[i % 2], 16)
                    if i + 2 < NF:
                        sp.dma_start(buf[:, i % 2, :], recon_dram[:, (i + 2) * FC:(i + 3) * FC])\
                            .then_inc(buf_in[i % 2], 16)
                for i in range(2):
                    sp.wait_ge(stored[i], 16 * (NF // 2))

            @block.tensor
            def _(pe):
                pe.wait_ge(agg_ready, 1)
                nc.tensor.matmul(ps[:, 0, 0:B], wt("group_mean"), gmean[:], start=True, stop=True).then_inc(gmean_mm, 1)
                pe.wait_ge(dev_ready, 1)
                nc.tensor.matmul(ps[:, 1, 0:B], wt("group_mean"), dev[:], start=True, stop=True).then_inc(gvar_mm, 1)

            @block.scalar
            def _(act):
                act.wait_ge(var_ready, 1)
                nc.scalar.activation(std[:], dev[:], ACT.Sqrt).then_inc(std_ready, 1)
                act.wait_ge(affine_ready, 1)
                for i in range(NF):
                    b = i * FC // N
                    act.wait_ge(buf_in[i % 2], 16 * (i // 2 + 1))
                    if i >= 2:
                        act.wait_ge(stored[i % 2], 16 * (i // 2))
                    nc.scalar.activation(res[:, i % 2, :], buf[:, i % 2, :], ACT.Silu, scale=scale[:, b:b + 1],
                                         bias=shift[:, b:b + 1]).then_inc(silu_done, 1)

            @block.vector
            def _(dve):
                for b in range(B):
                    nc.vector.bn_aggr(agg[:, b, :], stats[:, b * NB:(b + 1) * NB, :])
                dve.drain()
                nc.vector.tensor_copy(gmean[:], agg[:, :, 0]).then_inc(agg_ready, 1)
                dve.wait_ge(gmean_mm, 1)
                nc.vector.tensor_copy(gmean[:], ps[:, 0, 0:B])
                dve.drain()
                nc.vector.tensor_tensor(dev[:], agg[:, :, 0], gmean[:], ALU.subtract)
                dve.drain()
                nc.vector.tensor_tensor(dev[:], dev[:], dev[:], ALU.mult)
                dve.drain()
                nc.vector.tensor_tensor(dev[:], dev[:], agg[:, :, 1], ALU.add).then_inc(dev_ready, 1)
                dve.wait_ge(gvar_mm, 1)
                nc.vector.tensor_scalar(dev[:], ps[:, 1, 0:B], 1e-5, None, ALU.add).then_inc(var_ready, 1)
                dve.wait_ge(std_ready, 1)
                nc.vector.reciprocal(scale[:], std[:])
                dve.drain()
                nc.vector.tensor_scalar(scale[:], scale[:], wt("gn_w"), None, ALU.mult)
                dve.drain()
                nc.vector.tensor_tensor(shift[:], scale[:], gmean[:], ALU.mult)
                dve.drain()
                nc.vector.tensor_scalar(shift[:], shift[:], -1.0, wt("gn_b"), ALU.mult, ALU.add).then_inc(affine_ready, 1)
                for i in range(NF):
                    dve.wait_ge(silu_done, i + 1)
                    nc.vector.tensor_tensor(res[:, i % 2, :], res[:, i % 2, :], xp[:, PAD + i * FC:PAD + (i + 1) * FC],
                                            ALU.add).then_inc(res_done, 1)


def network(nc, x_in, w0, w1, conv1, w2, w3, conv3, select, out):
    with ExitStack() as ctx:
        sb = lambda name, shape, dt=F32: ctx.enter_context(nc.sbuf_tensor(name, shape, dt))
        sem = lambda name: ctx.enter_context(nc.semaphore(name))
        xp = sb("xp", [128, B * N + 2 * PAD])
        x = xp[:, PAD:PAD + B * N]
        sel = sb("sel", [PARTS * SEL, SEL * 128], BF16)
        first_in = sem("first_in"); rest_in = sem("rest_in")
        w_in = [sem(f"w{layer}_in") for layer in range(4)]
        w1_sb = sb("w1_sb", [128, L1_WIDTH])
        w2_sb = sb("w2_sb", [128, L2_WIDTH])
        with nc.sbuf_tensor("w0_sb", [128, L0_WIDTH], F32) as w0_sb:
            with nc.Block() as block:

                @block.sync
                def _(sp):
                    samples = x_in.rearrange("b c h w -> c b (h w)")
                    sp.dma_start(x[:, 0:N], samples[:, 0, :]).then_inc(first_in, 16)
                    sp.dma_start(w0_sb[:], w0).then_inc(w_in[0], 16)
                    sp.dma_start(x[:, N:].rearrange("c (b n) -> c b n", b=B - 1), samples[:, 1:, :]).then_inc(rest_in, 16)
                    sp.dma_start(w1_sb[:], w1).then_inc(w_in[1], 16)
                    sp.dma_start(sel[:], select).then_inc(w_in[1], 16)
                    sp.dma_start(w2_sb[:], w2).then_inc(w_in[2], 16)

                @block.vector
                def _(dve):
                    nc.vector.memset(xp[:, 0:PAD], 0.0)
                    nc.vector.memset(xp[:, PAD + B * N:], 0.0)
                    dve.drain()

            sparse_attention_layer(nc, x, w0_sb, w_in[0], first_in, rest_in)
        scan_layer(nc, x, w1_sb, sel, w_in[1], conv1)
        w3_sb = sb("w3_sb", [128, L3_WIDTH])
        conv3_sb = sb("conv3_sb", [128, K3 * DI])
        rank_one_attention_layer(nc, x, w2_sb, w_in[2], [(w3_sb[:], w3, w_in[3]), (conv3_sb[:], conv3, w_in[3])])
        two_way_scan_layer(nc, xp, w3_sb, conv3_sb, sel, w_in[3], out)



def packed(at, width, entries):
    w = _np.zeros((128, width), _np.float32)
    for name, shift, block in entries:
        first = at[name].start + shift
        w[:block.shape[0], first:first + block.shape[1]] = block
    return w


def column(a):
    return a[:, None]


def rows(a, n=128):
    return _np.broadcast_to(a[None, :], (n, a.shape[0]))


def layer0_arrays(q_w, q_b, v_w, v_b, lw1_w, lw1_b, lw2_w, lw2_b, bw1_w, bw1_b, bw2_w, bw2_b, lin_w, lin_b):
    return packed(L0_AT, L0_WIDTH, [
        ("q_w", 0, q_w.T), ("v_w", 0, v_w.T), ("branch_w1", 0, lw1_w.T), ("branch_w1", MID, bw1_w.T),
        ("branch_w2", 0, _np.concatenate([lw2_w.T, _np.zeros((MID, 1))])),
        ("branch_w2", 1, _np.concatenate([_np.zeros((MID, 1)), bw2_w.T])),
        ("lin_w", 0, lin_w.transpose(1, 2, 3, 0).reshape(C, 9 * C)), ("v_b", 0, rows(v_b)), ("q_b", 0, column(q_b)),
        ("branch_b1", 0, column(_np.concatenate([lw1_b, bw1_b]))), ("branch_b2", 0, rows(lw2_b)),
        ("branch_b2", 1, rows(bw2_b)), ("lin_b", 0, column(lin_b)), ("ident", 0, _np.eye(128)),
        ("ones", 0, _np.ones((128, C)))])


def layer1_arrays(W_in, K_conv, b_conv, gamma, beta, W_dt, b_dt, W_dtr, b_dtr, A_log, D_param, W_out):
    w = packed(L1_AT, L1_WIDTH, [
        ("in_w", 0, W_in[:, :C]), ("dt_w", 0, W_dt[:, :R1]), ("bc_w", 0, W_dt[:, R1:]), ("dtr_w", 0, W_dtr),
        ("out_w", 0, W_out), ("ident", 0, _np.eye(128)), ("ones", 0, _np.ones((128, C))), ("A", 0, A_log),
        ("conv_b", 0, column(b_conv)), ("gamma", 0, column(gamma)), ("beta", 0, column(beta)),
        ("dt_b", 0, column(b_dt[:R1])), ("bc_b", 0, column(b_dt[R1:])), ("dtr_b", 0, column(b_dtr)),
        ("D", 0, column(D_param))])
    taps = rows(K_conv[:, 0].transpose(1, 2, 0).reshape(9 * C))
    return w, _np.concatenate([W_in[:, C:], taps], 1)


def layer2_arrays(Wf, bf, Wg, bg, Wh, bh):
    return packed(L2_AT, L2_WIDTH, [("h_w", 0, Wh.T), ("f_w", 0, Wf.T), ("g_w", 0, Wg.T), ("h_b", 0, rows(bh)),
                                    ("f_b", 0, rows(bf)), ("g_b", 0, rows(bg))])


def layer3_arrays(Win, conv_w, conv_b, Wx, Wdt, bdt, A_log, D, Wout, gn_w, gn_b):
    entries = [("u_w", 0, Win[:DI].T), ("z_w", 0, Win[DI:].T), ("gn_w", 0, column(gn_w)),
               ("gn_b", 0, column(gn_b)), ("ident", 0, _np.eye(128))]
    for e in range(TI):
        own = slice(e * 128, (e + 1) * 128)
        for a in range(PARTS):
            entries.append(("bc_w", e * (DT_AT + R3) + a * SEL, Wx[R3:, own].T))
        entries += [("bc_w", e * (DT_AT + R3) + DT_AT, Wx[:R3, own].T), ("out_w", e * 128, Wout[:, own].T), ("A", e * S3, A_log[own]),
                    ("conv_b", e, column(conv_b[own])), ("dtr_b", e, column(bdt[own])), ("D", e, column(D[own]))]
    group_mean = _np.zeros((C, C), _np.float32)
    for first in range(0, C, GROUP):
        group_mean[first:first + GROUP, first:first + GROUP] = 1 / GROUP
    below_top = _np.zeros((128, 2), _np.float32)
    below_top[SEL:3 * SEL, 0] = -1
    below_top[2 * SEL:3 * SEL, 1] = -1
    low_rank = _np.zeros((128, DI), _np.float32)
    low_rank[DT_AT:DT_AT + R3] = Wdt.T
    entries += [("dtr_w", 0, low_rank), ("group_mean", 0, group_mean), ("below_top", 0, below_top)]
    return packed(L3_AT, L3_WIDTH, entries), rows(conv_w[:, 0].T.reshape(K3 * DI))


def one_hot_rows():
    select = _np.zeros((PARTS * SEL, SEL, 128), _np.float32)
    for a in range(PARTS):
        for i in range(SEL):
            select[a * SEL + i, i, :] = 1
    return select.reshape(PARTS * SEL, SEL * 128).astype(mybir.dt.np(BF16))


def kernel(**inputs):
    import concourse.bacc as _bacc
    from concourse.bass_utils import run_bass_kernel_spmd as _run

    own = lambda layer: {k[len(layer) + 1:]: _np.asarray(v) for k, v in inputs.items() if k.startswith(layer)}
    w1, conv1 = layer1_arrays(**own("L1_conv"))
    w3, conv3 = layer3_arrays(**own("L3_conv"))
    arrays = {"x_in": _np.asarray(inputs["x"]), "w0": layer0_arrays(**own("L0_conv")), "w1": w1, "conv1": conv1,
              "w2": layer2_arrays(**own("L2_conv")), "w3": w3, "conv3": conv3, "one_hots": one_hot_rows()}
    arrays = {name: _np.ascontiguousarray(a) for name, a in arrays.items()}
    nc = _bacc.Bacc("TRN2", target_bir_lowering=False, num_devices=1)
    args = [nc.dram_tensor(name, a.shape, mybir.dt.from_np(a.dtype), kind="ExternalInput").ap()
            for name, a in arrays.items()]
    out = nc.dram_tensor("out", (B, C, H, W), F32, kind="ExternalOutput").ap()
    network(nc, *args, out)
    result = _run(nc, [arrays], core_ids=[0])
    return result.results[0]["out"]
```
